# Optimizing a Trainium2 kernel written in Bass

```python
import numpy as np
import jax
import jax.numpy as jnp

def _softmax(x, axis=-1):
    return jax.nn.softmax(x, axis=axis)

def _gelu(x):
    return jax.nn.gelu(x, approximate=True)

def _silu(x):
    return jax.nn.silu(x)

def _sigmoid(x):
    return jax.nn.sigmoid(x)

def _layernorm(x, axis=-1, eps=1e-05):
    m = jnp.mean(x, axis=axis, keepdims=True)
    v = jnp.var(x, axis=axis, keepdims=True)
    return (x - m) / jnp.sqrt(v + eps)

def _scatter_add(tgt, idx, src, axis=0):
    return tgt.at[idx].add(src)

def _segment_sum(src, seg, n):
    return jax.ops.segment_sum(src, seg, n)
kernel_name = 'mk_macaron_d1_jaxref_r8_55cd96'

def setup_inputs(seed: int=0):
    np.random.seed(seed)
    _w = jnp.asarray

    def _L0_attn_setup():
        import jax, jax.numpy as jnp
        import numpy as np
        DIM = 128
        HEADS = 16
        DIM_HEAD = 64
        NUM_FREQS = 16
        INNER = HEADS * DIM_HEAD

        def rotate_half(x):
            x1 = x[..., ::2]
            x2 = x[..., 1::2]
            return jnp.concatenate((-x2, x1), axis=-1)

        def rope_fourier_cache(seq_len, head_dim, num_freqs):
            freqs = 10000.0 ** (-jnp.arange(0, head_dim, 2, dtype=jnp.float32) / head_dim)
            pos = jnp.arange(seq_len, dtype=jnp.float32)[:, None]
            angles = pos * freqs
            sin = jnp.sin(angles)
            cos = jnp.cos(angles)
            sin = jnp.stack([sin, sin], axis=-1).reshape(seq_len, head_dim)
            cos = jnp.stack([cos, cos], axis=-1).reshape(seq_len, head_dim)
            ffreqs = jnp.arange(1, num_freqs + 1, dtype=jnp.float32)
            p = jnp.arange(seq_len, dtype=jnp.float32)[:, None]
            fourier = jnp.concatenate([jnp.sin(p * ffreqs), jnp.cos(p * ffreqs)], axis=-1)
            return (sin, cos, fourier)
        key = jax.random.key(seed)
        ks = jax.random.split(key, 6)
        b, n = (4, 256)
        x = jax.random.normal(ks[0], (b, n, DIM), dtype=jnp.float32)
        w_qkv = jax.random.normal(ks[1], (3 * INNER, DIM), dtype=jnp.float32) * DIM ** (-0.5)
        w_fproj = jax.random.normal(ks[2], (DIM_HEAD, 2 * NUM_FREQS), dtype=jnp.float32) * (2 * NUM_FREQS) ** (-0.5)
        b_fproj = jax.random.normal(ks[3], (DIM_HEAD,), dtype=jnp.float32) * 0.02
        w_out = jax.random.normal(ks[4], (DIM, INNER), dtype=jnp.float32) * INNER ** (-0.5)
        b_out = jax.random.normal(ks[5], (DIM,), dtype=jnp.float32) * 0.02
        return {'x': x, 'w_qkv': w_qkv, 'w_fproj': w_fproj, 'b_fproj': b_fproj, 'w_out': w_out, 'b_out': b_out}
    _L0_attn_in = _L0_attn_setup()

    def _L0_ffn_setup():
        import math
        import jax, jax.numpy as jnp
        import numpy as np
        B, S, H = (4, 256, 128)
        E, K, I = (8, 2, 128)
        NSH = 2
        CF, RSF = (1.25, 1.0)
        key = jax.random.key(seed)
        ks = jax.random.split(key, 8)
        w = lambda k, sh: jax.random.normal(k, sh, dtype=jnp.float32) * 0.02
        return {'hidden_states': jax.random.normal(ks[0], (B, S, H), dtype=jnp.float32), 'gate_w': w(ks[1], (E, H)), 'we_gate': w(ks[2], (E, I, H)), 'we_up': w(ks[3], (E, I, H)), 'we_down': w(ks[4], (E, H, I)), 'ws_gate': w(ks[5], (NSH * I, H)), 'ws_up': w(ks[6], (NSH * I, H)), 'ws_down': w(ks[7], (H, NSH * I))}
    _L0_ffn_in = _L0_ffn_setup()
    _d = {'L0_attn_x': _L0_attn_in['x'], 'L0_attn_w_qkv': _L0_attn_in['w_qkv'], 'L0_attn_w_fproj': _L0_attn_in['w_fproj'], 'L0_attn_b_fproj': _L0_attn_in['b_fproj'], 'L0_attn_w_out': _L0_attn_in['w_out'], 'L0_attn_b_out': _L0_attn_in['b_out'], 'L0_ffn_gate_w': _L0_ffn_in['gate_w'], 'L0_ffn_we_gate': _L0_ffn_in['we_gate'], 'L0_ffn_we_up': _L0_ffn_in['we_up'], 'L0_ffn_we_down': _L0_ffn_in['we_down'], 'L0_ffn_ws_gate': _L0_ffn_in['ws_gate'], 'L0_ffn_ws_up': _L0_ffn_in['ws_up'], 'L0_ffn_ws_down': _L0_ffn_in['ws_down']}
    _x0 = _d['L0_attn_x']
    _d['L0_attn_x'] = jax.random.normal(jax.random.fold_in(jax.random.key(seed), 1), (8, 512, 128), dtype=_x0.dtype)
    del _x0
    return _d

def reference(L0_attn_x, L0_attn_w_qkv, L0_attn_w_fproj, L0_attn_b_fproj, L0_attn_w_out, L0_attn_b_out, L0_ffn_gate_w, L0_ffn_we_gate, L0_ffn_we_up, L0_ffn_we_down, L0_ffn_ws_gate, L0_ffn_ws_up, L0_ffn_ws_down):

    def _L0_attn_ref(x, w_qkv, w_fproj, b_fproj, w_out, b_out):
        import jax, jax.numpy as jnp
        import numpy as np
        DIM = 128
        HEADS = 16
        DIM_HEAD = 64
        NUM_FREQS = 16
        INNER = HEADS * DIM_HEAD

        def rotate_half(x):
            x1 = x[..., ::2]
            x2 = x[..., 1::2]
            return jnp.concatenate((-x2, x1), axis=-1)

        def rope_fourier_cache(seq_len, head_dim, num_freqs):
            freqs = 10000.0 ** (-jnp.arange(0, head_dim, 2, dtype=jnp.float32) / head_dim)
            pos = jnp.arange(seq_len, dtype=jnp.float32)[:, None]
            angles = pos * freqs
            sin = jnp.sin(angles)
            cos = jnp.cos(angles)
            sin = jnp.stack([sin, sin], axis=-1).reshape(seq_len, head_dim)
            cos = jnp.stack([cos, cos], axis=-1).reshape(seq_len, head_dim)
            ffreqs = jnp.arange(1, num_freqs + 1, dtype=jnp.float32)
            p = jnp.arange(seq_len, dtype=jnp.float32)[:, None]
            fourier = jnp.concatenate([jnp.sin(p * ffreqs), jnp.cos(p * ffreqs)], axis=-1)
            return (sin, cos, fourier)
        b, n, _ = x.shape
        scale = DIM_HEAD ** (-0.5)
        qkv = x @ w_qkv.T
        q, k, v = jnp.split(qkv, 3, axis=-1)

        def to_heads(t):
            return t.reshape(b, n, HEADS, DIM_HEAD).transpose(0, 2, 1, 3)
        q, k, v = (to_heads(q), to_heads(k), to_heads(v))
        sin, cos, fourier = rope_fourier_cache(n, DIM_HEAD, NUM_FREQS)
        fenc = fourier @ w_fproj.T + b_fproj
        fenc = fenc[None, None]
        q = q * cos + rotate_half(q) * sin + fenc
        k = k * cos + rotate_half(k) * sin + fenc
        dots = jnp.einsum('bhid,bhjd->bhij', q, k) * scale
        attn = jax.nn.softmax(dots, axis=-1)
        out = jnp.einsum('bhij,bhjd->bhid', attn, v)
        out = out.transpose(0, 2, 1, 3).reshape(b, n, INNER)
        return out @ w_out.T + b_out

    def _L0_ffn_ref(hidden_states, gate_w, we_gate, we_up, we_down, ws_gate, ws_up, ws_down):
        import math
        import jax, jax.numpy as jnp
        import numpy as np
        B, S, H = (4, 256, 128)
        E, K, I = (8, 2, 128)
        NSH = 2
        CF, RSF = (1.25, 1.0)
        orig_shape = hidden_states.shape
        x = hidden_states.reshape(-1, H)
        N = x.shape[0]
        logits = x.astype(jnp.float32) @ gate_w.astype(jnp.float32).T
        scores = jax.nn.softmax(logits, axis=-1)
        topk_w, topk_idx = jax.lax.top_k(scores, K)
        topk_w = topk_w / (topk_w.sum(-1, keepdims=True) + 1e-20) * RSF
        capacity = math.ceil(CF * N * K / E)
        flat = topk_idx.reshape(-1)
        one_hot = jax.nn.one_hot(flat, E, dtype=jnp.int32)
        pos = jnp.cumsum(one_hot, axis=0) - 1
        pos_tok = jnp.take_along_axis(pos, flat[:, None], axis=1)[:, 0]
        keep = (pos_tok < capacity).reshape(N, K)
        topk_w = topk_w * keep.astype(topk_w.dtype)
        comb = jnp.zeros((N, E), jnp.float32).at[jnp.arange(N)[:, None], topk_idx].add(topk_w)
        g = jnp.einsum('nh,eih->nei', x, we_gate)
        u = jnp.einsum('nh,eih->nei', x, we_up)
        eo = jnp.einsum('nei,ehi->neh', jax.nn.silu(g) * u, we_down)
        y = jnp.einsum('neh,ne->nh', eo, comb)
        sh = jax.nn.silu(x @ ws_gate.T) * (x @ ws_up.T) @ ws_down.T
        return (y + sh).reshape(orig_shape)
    x = L0_attn_x
    x = x + 0.5 * _L0_ffn_ref(_layernorm(x, axis=-1), L0_ffn_gate_w, L0_ffn_we_gate, L0_ffn_we_up, L0_ffn_we_down, L0_ffn_ws_gate, L0_ffn_ws_up, L0_ffn_ws_down)
    x = x + _L0_attn_ref(_layernorm(x, axis=-1), L0_attn_w_qkv, L0_attn_w_fproj, L0_attn_b_fproj, L0_attn_w_out, L0_attn_b_out)
    x = x + 0.5 * _L0_ffn_ref(_layernorm(x, axis=-1), L0_ffn_gate_w, L0_ffn_we_gate, L0_ffn_we_up, L0_ffn_we_down, L0_ffn_ws_gate, L0_ffn_ws_up, L0_ffn_ws_down)
    return x

_drawn_inputs = setup_inputs


def setup_inputs(seed=0):
    import zlib

    import numpy as np

    out = dict(_drawn_inputs(seed))
    spreads = {}
    factors = {'L0_attn_b_fproj': 8.0,
     'L0_ffn_gate_w': 8.0,
     'L0_ffn_we_gate': 8.0,
     'L0_ffn_we_up': 8.0,
     'L0_ffn_we_down': 8.0,
     'L0_ffn_ws_gate': 7.103,
     'L0_ffn_ws_up': 7.023,
     'L0_ffn_ws_down': 7.053,
     'L0_attn_b_out': 2.684}
    for name, (base, spread) in spreads.items():
        noise = np.random.default_rng([zlib.crc32(name.encode()), seed]).standard_normal(out[name].shape)
        drawn = base * np.exp(spread * noise) if base else spread * noise
        out[name] = jnp.asarray(drawn.astype(out[name].dtype))
    for name, factor in factors.items():
        out[name] = (out[name] * factor).astype(out[name].dtype)
    return out
```

```python
from contextlib import ExitStack

import concourse.bass as bass
from concourse import mybir

F32 = mybir.dt.float32
F32R = mybir.dt.float32r
BF16 = mybir.dt.bfloat16
I32 = mybir.dt.int32
ALU = mybir.AluOpType
ACT = mybir.ActivationFunctionType
AX = mybir.AxisListType

P = 128
B, T, D = 8, 512, 128
TT = T // P
HEADS, DH = 16, 64
INNER = HEADS * DH
PAIRS = HEADS // 2
NF = 32
E, NSH, TOPK = 8, 2, 2
GROUPS = NSH + E
CAPACITY = -(-5 * B * T * TOPK // (4 * E))
EPS = 1e-5
QSCALE = DH ** -0.5
UNITS = 2 * TT
PARTS = 4
LAG = 3
NP = 4
SPLIT3 = 3
EVAC_ON_DVE = (1, 4, 6)
DVE_EV, ACT_EV = len(EVAC_ON_DVE), UNITS - len(EVAC_ON_DVE)
RSQRT_MAGIC = 0x5F3759DF
NEWTON = 4
LN_STEPS = TT + 7 + 2 + 4 * NEWTON + TT - 1


class Steps:

    def __init__(self, eng, sem, base=0):
        self.eng, self.sem, self.base, self.n = eng, sem, base, 0

    def link(self, ins):
        ins.then_inc(self.sem, 1)
        self.n += 1
        self.eng.wait_ge(self.sem, self.base + self.n)

    def mark(self, ins):
        ins.then_inc(self.sem, 1)
        self.n += 1


def macaron(nc, x, w_gate_up, w_down, gate_t, w_qk, w_v, w_out, b_out, fproj, bproj,
            rope, fourier, consts, consts_b, sel, out):
    with ExitStack() as ctx:
        def sb(name, shape, dt=F32):
            return ctx.enter_context(nc.sbuf_tensor(name, shape, dt))

        def sem(name):
            return ctx.enter_context(nc.semaphore(name))

        x_tok = sb("x_tok", [P, B, TT, D])
        gu_hi = sb("gu_hi", [P, 2 * GROUPS, P], F32R)
        gu_lo = sb("gu_lo", [P, 2 * GROUPS, P], F32R)
        down = sb("down", [P, GROUPS, D])
        gate_w = sb("gate_w", [P, E])
        gate_hi = sb("gate_hi", [P, E], F32R)
        gate_lo = sb("gate_lo", [P, E], F32R)
        qk_hi = sb("qk_hi", [P, PAIRS, PARTS, P], F32R)
        qk_lo = sb("qk_lo", [P, PAIRS, PARTS, P], F32R)
        v_hi = sb("v_hi", [P, INNER], F32R)
        v_lo = sb("v_lo", [P, INNER], F32R)
        wo = sb("wo", [P, PAIRS, D])
        bo = sb("bo", [P, 1])
        rope_t = sb("rope_t", [P, PARTS, T])
        fenc = sb("fenc", [P, 2, T])
        ident = sb("ident", [P, P])
        ident_b = sb("ident_b", [P, P], BF16)
        before_b = sb("before_b", [P, P], BF16)
        ones_b = sb("ones_b", [P, P], BF16)
        lower = sb("lower", [P, E, E])
        sel_b = sb("sel_b", [P, E, P], BF16)
        x_hi = sb("x_hi", [P, T], F32R)
        x_lo = sb("x_lo", [P, T], F32R)
        xn = sb("xn", [P, TT, D])
        y_t = sb("y_t", [P, T])
        stats = sb("stats", [P, TT, 6])
        mv = sb("mv", [P, TT, 2])
        mean = sb("mean", [P, TT])
        ve = sb("ve", [P, TT])
        rs = sb("rs", [P, TT])
        rsi = sb("rsi", [P, TT], I32)
        nt = sb("nt", [P, 2, TT])
        work = sb("work", [P, 3 * 4096])
        v_all = work[:, 0:4096].rearrange("p (t n) -> p t n", t=TT)
        pt = work[:, 4096:].rearrange("p (g h k q) -> p g h k q", g=2, h=2, k=TT)
        st_qk = work[:, 0:PAIRS * PARTS * P]
        st_v = work[:, 4096:4096 + INNER]
        st_gu = work[:, 4096 + INNER:4096 + INNER + 2 * GROUPS * P]
        prob = sb("prob", [P, NP, T])
        act_g, prod = prob[:, 0:2, :], prob[:, 2:4, :]
        hid = sb("hid", [P, 2, T])
        o_t = hid
        comb_t = sb("comb_t", [P, T], BF16)
        route = sb("route", [P, 8, TT, E])
        pair_gt = sb("pair_gt", [P, TT, E, E])
        pair_ge = sb("pair_ge", [P, TT, E, E])
        small = sb("small", [P, 8, TT])
        mask_b = sb("mask_b", [P, TT, E], BF16)
        count_b = sb("count_b", [P, E], BF16)
        count = sb("count", [P, E])
        tile_n = sb("tile_n", [P, E])
        comb3 = sb("comb3", [P, TT, SPLIT3, E], BF16)
        q_pad = sb("q_pad", [P, 2, 2, T])
        k_rot = sb("k_rot", [P, 2, T])
        rope_tmp = sb("rope_tmp", [P, 2, PARTS, T])
        neg_max = sb("neg_max", [P, 2, UNITS])
        den = sb("den", [P, 2, UNITS])
        rec = sb("rec", [P, 3, UNITS])
        rec3 = sb("rec3", [P, 2, SPLIT3, 2, TT], BF16)
        rec_all = sb("rec_all", [P, T])
        fourier_s = sb("fourier_s", [NF, T])
        fproj_s = sb("fproj_s", [NF, P])
        bproj_s = sb("bproj_s", [P, 1])

        bank = [ctx.enter_context(nc.psum_tensor(f"bank{i}", [P, T], F32)) for i in range(8)]

        in_x, in_ffn, in_att, in_small = sem("in_x"), sem("in_ffn"), sem("in_att"), sem("in_small")
        consts_ready = sem("consts_ready")
        w_hi_ready, w_lo_ready = sem("w_hi_ready"), sem("w_lo_ready")
        fenc_ps, fenc_ready = sem("fenc_ps"), sem("fenc_ready")
        dve_step = {ph: sem(f"dve_step_{ph}") for ph in ("setup", "f1", "att", "f2")}
        stored = sem("stored")

        block = ctx.enter_context(nc.Block())
        progs = {e: [] for e in ("sync", "scalar", "vector", "tensor", "gpsimd")}

        def setup_sync(sp):
            sp.dma_start(x_tok[:, 0], x[0].rearrange("(t p) d -> p t d", p=P)).then_inc(in_x, 16)
            sp.dma_start(gate_w[:], gate_t).then_inc(in_small, 16)
            sp.dma_start(ident[:], consts[0]).then_inc(in_small, 16)
            sp.dma_start(st_gu, w_gate_up).then_inc(in_ffn, 16)
            sp.dma_start(down[:].rearrange("p g d -> p (g d)"), w_down).then_inc(in_ffn, 16)
            for b in range(1, B):
                sp.dma_start(x_tok[:, b], x[b].rearrange("(t p) d -> p t d", p=P)).then_inc(in_x, 16)
            sp.dma_start(st_qk, w_qk).then_inc(in_att, 16)
            sp.dma_start(st_v, w_v).then_inc(in_att, 16)
            sp.dma_start(wo[:].rearrange("p g d -> p (g d)"), w_out).then_inc(in_att, 16)

        def setup_act(act):
            act.dma_start(before_b[:], consts_b[0]).then_inc(in_small, 16)
            act.dma_start(ident_b[:], consts_b[1]).then_inc(in_small, 16)
            act.dma_start(sel_b[:].rearrange("p e m -> p (e m)"), sel).then_inc(in_small, 16)
            act.dma_start(lower[:].rearrange("p a b -> p (a b)"), consts[1][:, 0:E * E]).then_inc(in_small, 16)
            act.dma_start(rope_t[:].rearrange("p a t -> p (a t)"), rope).then_inc(in_small, 16)
            act.dma_start(fourier_s[:], fourier).then_inc(in_small, 16)
            act.dma_start(fproj_s[:], fproj).then_inc(in_small, 16)
            act.dma_start(bproj_s[:], bproj).then_inc(in_small, 16)
            act.dma_start(bo[:], b_out).then_inc(in_small, 16)
            act.wait_ge(in_small, 11 * 16)
            nc.scalar.activation(gate_hi[:], gate_w[:], ACT.Copy).then_inc(w_hi_ready, 1)
            act.wait_ge(in_ffn, 32)
            nc.scalar.activation(gu_hi[:].rearrange("p g n -> p (g n)"), st_gu, ACT.Copy).then_inc(w_hi_ready, 1)
            act.wait_ge(in_att, 48)
            nc.scalar.activation(qk_hi[:].rearrange("p a b n -> p (a b n)"), st_qk, ACT.Copy).then_inc(w_hi_ready, 1)
            nc.scalar.activation(v_hi[:], st_v, ACT.Copy).then_inc(w_hi_ready, 1)
            act.wait_ge(fenc_ps, 1)
            nc.scalar.activation(fenc[:, 1, :], bank[7][:], ACT.Identity, bias=bproj_s[:, 0:1]).then_inc(fenc_ready, 1)
            act.wait_ge(fenc_ready, 1)
            nc.scalar.activation(fenc[:, 0, :], fenc[:, 1, :], ACT.Copy, scale=QSCALE).then_inc(fenc_ready, 1)

        def setup_dve(dve):
            nc.vector.memset(ones_b[:], 1.0).then_inc(consts_ready, 1)
            nc.vector.memset(comb_t[:], 0.0).then_inc(consts_ready, 1)
            dve.wait_ge(w_hi_ready, 1)
            nc.vector.tensor_tensor(gate_lo[:], gate_w[:], gate_hi[:], ALU.subtract).then_inc(w_lo_ready, 1)
            dve.wait_ge(w_hi_ready, 2)
            nc.vector.tensor_tensor(gu_lo[:].rearrange("p g n -> p (g n)"), st_gu,
                                    gu_hi[:].rearrange("p g n -> p (g n)"), ALU.subtract).then_inc(w_lo_ready, 1)
            dve.wait_ge(w_hi_ready, 4)
            nc.vector.tensor_tensor(qk_lo[:].rearrange("p a b n -> p (a b n)"), st_qk,
                                    qk_hi[:].rearrange("p a b n -> p (a b n)"), ALU.subtract).then_inc(w_lo_ready, 1)
            nc.vector.tensor_tensor(v_lo[:], st_v, v_hi[:], ALU.subtract).then_inc(w_lo_ready, 1)

        def setup_pe(pe):
            pe.wait_ge(in_small, 11 * 16)
            nc.tensor.matmul(bank[7][:], fproj_s[:], fourier_s[:], start=True, stop=True).then_inc(fenc_ps, 1)

        def setup_pool(pool):
            nc.gpsimd.memset(q_pad[:], 0.0).then_inc(consts_ready, 1)

        def layer_norm(dve, steps, xb):
            for t in range(TT):
                steps.mark(nc.vector.bn_stats(stats[:, t, :], xb(t)))
            dve.wait_ge(steps.sem, steps.base + steps.n)
            even, odd = stats[:, :, 0:3], stats[:, :, 3:6]
            steps.mark(nc.vector.tensor_tensor(mv[:, :, 0], even[:, :, 1], odd[:, :, 1], ALU.add))
            steps.mark(nc.vector.tensor_tensor(mv[:, :, 1], even[:, :, 1], odd[:, :, 1], ALU.subtract))
            steps.link(nc.vector.tensor_tensor(ve[:], even[:, :, 2], odd[:, :, 2], ALU.add))
            steps.mark(nc.vector.tensor_scalar(mean[:], mv[:, :, 0], 0.5, None, ALU.mult))
            steps.mark(nc.vector.tensor_scalar(rs[:], ve[:], 1.0 / D, EPS, ALU.mult, ALU.add))
            steps.link(nc.vector.tensor_tensor(nt[:, 0, :], mv[:, :, 1], mv[:, :, 1], ALU.mult))
            steps.link(nc.vector.scalar_tensor_tensor(ve[:], nt[:, 0, :], 0.25, rs[:], ALU.mult, ALU.add))
            steps.link(nc.vector.tensor_scalar(rsi[:], ve[:].bitcast(I32), 1, None, ALU.logical_shift_right))
            steps.link(nc.vector.tensor_scalar(rs[:].bitcast(I32), rsi[:], -1, RSQRT_MAGIC, ALU.mult, ALU.add))
            for _ in range(NEWTON):
                steps.link(nc.vector.tensor_tensor(nt[:, 0, :], rs[:], rs[:], ALU.mult))
                steps.link(nc.vector.tensor_tensor(nt[:, 1, :], nt[:, 0, :], ve[:], ALU.mult))
                steps.link(nc.vector.tensor_scalar(nt[:, 0, :], nt[:, 1, :], -0.5, 1.5, ALU.mult, ALU.add))
                steps.link(nc.vector.tensor_tensor(rs[:], rs[:], nt[:, 0, :], ALU.mult))
            for t in range(TT):
                last = nc.vector.tensor_scalar(xn[:, t, :], xb(t), mean[:, t:t + 1], rs[:, t:t + 1],
                                               ALU.subtract, ALU.mult)
                if t < TT - 1:
                    steps.mark(last)
            return last

        def ffn(tag, last):
            s = {n: sem(f"{tag}_{n}") for n in (
                "xn_ready", "xt_ps", "x_hi_ready", "x_lo_ready", "logits", "shifted", "exps", "masks", "pos",
                "comb_parts", "comb_ps", "comb_ready", "gu_ps", "silu", "gated", "weight_ps", "hidden",
                "y_ps", "y_copied", "yt_ps", "x_done")}
            G, U, C = (bank[0], bank[1]), (bank[2], bank[3]), (bank[4], bank[5])
            Y, M = bank[6], bank[7]
            M_log = M[:, 0:TT * E]
            M_comb = M[0:SPLIT3 * E, 0:T // 2].bitcast(BF16)
            step_sem = dve_step[tag]
            LN = LN_STEPS
            RT = 21

            def pe_front(pe):
                for t in range(TT):
                    ins = nc.tensor.transpose(M[:, t * P:(t + 1) * P], xn[:, t, :], ident[:])
                ins.then_inc(s["xt_ps"], 1)

            def pe(pe):
                pe.wait_ge(s["xn_ready"], 1)
                if tag == "f1":
                    pe.wait_ge(fenc_ready, 1)
                    pe.wait_ge(consts_ready, 3)
                pe_front(pe)
                with pe.Fori(0, B) as b:
                    pe.wait_ge(s["x_hi_ready"], b + 1)
                    pe.wait_ge(s["x_lo_ready"], b + 1)
                    pe.wait_ge(w_lo_ready, 2)
                    for t in range(TT):
                        tok = slice(t * P, (t + 1) * P)
                        for n, (a, w) in enumerate(((x_hi, gate_hi), (x_lo, gate_hi), (x_hi, gate_lo))):
                            ins = nc.tensor.matmul(M[:, t * E:(t + 1) * E], a[:, tok], w[:],
                                                   start=(n == 0), stop=(n == 2))
                    ins.then_inc(s["logits"], 1)

                    def gate_up(k):
                        if k >= 2:
                            pe.wait_ge(s["gated"], b * GROUPS + (k - 1))
                        for dst, j in ((G[k % 2], 0), (U[k % 2], GROUPS)):
                            for n, (w, a) in enumerate(((gu_hi, x_hi), (gu_lo, x_hi), (gu_hi, x_lo))):
                                ins = nc.tensor.matmul(dst[:], w[:, j + k, :], a[:], start=(n == 0), stop=(n == 2))
                        ins.then_inc(s["gu_ps"], 1)

                    def weights(k):
                        e = k - NSH
                        if e == 0:
                            pe.wait_ge(s["comb_ready"], b + 1)
                        if e >= 2:
                            pe.wait_ge(s["hidden"], b * E + (e - 1))
                        nc.tensor.matmul(C[k % 2][:], sel_b[:, e, :], comb_t[:],
                                         start=True, stop=True).then_inc(s["weight_ps"], 1)

                    def project(k):
                        if k < NSH:
                            pe.wait_ge(s["gated"], b * GROUPS + (k + 1))
                        else:
                            pe.wait_ge(s["hidden"], b * E + (k - NSH + 1))
                        nc.tensor.matmul(Y[:], down[:, k, :], hid[:, k % 2, :], start=(k == 0),
                                         stop=(k == GROUPS - 1)).then_inc(s["y_ps"], 1)

                    for k in range(GROUPS):
                        gate_up(k)
                        if k == 1:
                            pe.wait_ge(s["masks"], b + 1)
                            nc.tensor.matmul(M_log, before_b[:], mask_b[:].rearrange("p t e -> p (t e)"),
                                             start=True, stop=False)
                            nc.tensor.matmul(M_log.rearrange("p (t e) -> p t e", e=E), ones_b[:],
                                             count_b[:].unsqueeze(1).broadcast_to([P, TT, E]),
                                             start=False, stop=False)
                            for t in range(TT - 1):
                                ins = nc.tensor.matmul(
                                    M[:, (t + 1) * E:TT * E].rearrange("p (t e) -> p t e", e=E), ones_b[:],
                                    mask_b[:, t:t + 1, :].broadcast_to([P, TT - 1 - t, E]),
                                    start=False, stop=(t == TT - 2))
                            ins.then_inc(s["pos"], 1)
                        if k == 2:
                            pe.wait_ge(s["comb_parts"], b + 1)
                            for t in range(TT):
                                ins = nc.tensor.transpose(M_comb[:, t * P:(t + 1) * P],
                                                          comb3[:, t, :, :].rearrange("p a e -> p (a e)"), ident_b[:])
                            ins.then_inc(s["comb_ps"], 1)
                        if k - 1 >= NSH:
                            weights(k - 1)
                        if k >= 2:
                            project(k - 2)
                        if k == GROUPS - 1:
                            pe.wait_ge(s["xn_ready"], b + 2)
                            pe_front(pe)
                    weights(GROUPS - 1)
                    project(GROUPS - 2)
                    project(GROUPS - 1)
                    pe.wait_ge(s["y_copied"], b + 1)
                    pe.wait_ge(s["x_hi_ready"], b + 2)
                    pe.wait_ge(s["x_lo_ready"], b + 2)
                    for t in range(TT):
                        ins = nc.tensor.transpose(M[:, t * P:(t + 1) * P], y_t[:, t * P:(t + 1) * P], ident[:])
                    ins.then_inc(s["yt_ps"], 1)
                    pe.wait_ge(s["x_done"], b + 1)

            def act(act):
                act.wait_ge(s["xt_ps"], 1)
                nc.scalar.activation(x_hi[:], M[:], ACT.Copy).then_inc(s["x_hi_ready"], 1)
                with act.Fori(0, B) as b:
                    act.wait_ge(s["shifted"], b + 1)
                    nc.scalar.activation(route[:, 1], route[:, 0], ACT.Exp).then_inc(s["exps"], 1)
                    for k in range(GROUPS):
                        act.wait_ge(s["gu_ps"], b * GROUPS + (k + 1))
                        if k >= 2:
                            act.wait_ge(s["gated"], b * GROUPS + (k - 1))
                        nc.scalar.activation(act_g[:, k % 2, :], G[k % 2][:], ACT.Silu).then_inc(s["silu"], 1)
                    act.wait_ge(s["xt_ps"], b + 2)
                    nc.scalar.activation(x_hi[:], M[:], ACT.Copy).then_inc(s["x_hi_ready"], 1)
                    act.wait_ge(s["y_ps"], (b + 1) * GROUPS)
                    nc.scalar.activation(y_t[:], Y[:], ACT.Copy, scale=0.5).then_inc(s["y_copied"], 1)

            def x_tile(b):
                return lambda t: x_tok[:, bass.ds(b, 1), t, :].rearrange("p a d -> p (a d)") \
                    if not isinstance(b, int) else x_tok[:, b, t, :]

            def dve(dve):
                if tag == "f1":
                    dve.wait_ge(in_x, 16)
                steps = Steps(dve, step_sem)
                layer_norm(dve, steps, x_tile(0)).then_inc(s["xn_ready"], 1)
                assert steps.n == LN, steps.n
                dve.wait_ge(s["x_hi_ready"], 1)
                nc.vector.tensor_tensor(x_lo[:], M[:], x_hi[:], ALU.subtract).then_inc(s["x_lo_ready"], 1)
                steps.link(nc.vector.memset(count[:], 0.0))
                steps.link(nc.vector.memset(count_b[:], 0.0))
                first = steps.n
                per = LN + RT
                with dve.Fori(0, B) as b:
                    steps = Steps(dve, step_sem, b * per + first)
                    big, small_t = (lambda n: route[:, n]), (lambda n: small[:, n, :])
                    per_e = lambda ap: ap.unsqueeze(2).broadcast_to([P, TT, E])
                    dve.wait_ge(s["logits"], b + 1)
                    logits = M_log.rearrange("p (t e) -> p t e", e=E)
                    steps.link(nc.vector.tensor_reduce(small_t(0), logits, AX.X, ALU.max))
                    nc.vector.tensor_tensor(big(0), logits, per_e(small_t(0)), ALU.subtract).then_inc(s["shifted"], 1)
                    dve.wait_ge(s["exps"], b + 1)
                    steps.link(nc.vector.tensor_reduce(small_t(1), big(1), AX.X, ALU.add))
                    steps.link(nc.vector.reciprocal(small_t(2), small_t(1)))
                    steps.link(nc.vector.tensor_tensor(big(2), big(1), per_e(small_t(2)), ALU.mult))
                    other = big(2).unsqueeze(2).broadcast_to([P, TT, E, E])
                    own = big(2).unsqueeze(3).broadcast_to([P, TT, E, E])
                    steps.mark(nc.vector.tensor_tensor(pair_gt[:], other, own, ALU.is_gt))
                    steps.link(nc.vector.tensor_tensor(pair_ge[:], other, own, ALU.is_ge))
                    steps.link(nc.vector.tensor_tensor(pair_ge[:], pair_ge[:],
                                                       lower[:].unsqueeze(1).broadcast_to([P, TT, E, E]), ALU.mult))
                    steps.link(nc.vector.tensor_tensor(pair_gt[:], pair_gt[:], pair_ge[:], ALU.max))
                    steps.link(nc.vector.tensor_reduce(big(3), pair_gt[:], AX.X, ALU.add))
                    nc.vector.tensor_scalar(mask_b[:], big(3), float(TOPK), None, ALU.is_lt).then_inc(s["masks"], 1)
                    dve.wait_ge(s["masks"], b + 1)
                    steps.link(nc.vector.tensor_tensor(big(4), big(2), mask_b[:], ALU.mult))
                    steps.link(nc.vector.tensor_reduce(small_t(3), big(4), AX.X, ALU.add))
                    steps.link(nc.vector.tensor_scalar(small_t(4), small_t(3), 1e-20, None, ALU.add))
                    steps.link(nc.vector.reciprocal(small_t(5), small_t(4)))
                    steps.link(nc.vector.tensor_tensor(big(5), big(4), per_e(small_t(5)), ALU.mult))

                    def gated(k):
                        dve.wait_ge(s["silu"], b * GROUPS + (k + 1))
                        if k >= NSH + 2:
                            dve.wait_ge(s["hidden"], b * E + (k - NSH - 1))
                        dst = hid if k < NSH else prod
                        ins = nc.vector.tensor_tensor(dst[:, k % 2, :], act_g[:, k % 2, :], U[k % 2][:], ALU.mult)
                        ins.then_inc(s["gated"], 1)

                    def weighted(k):
                        dve.wait_ge(s["weight_ps"], b * E + (k - NSH + 1))
                        dve.wait_ge(s["gated"], b * GROUPS + (k + 1))
                        dve.wait_ge(s["y_ps"], b * GROUPS + (k - 1))
                        nc.vector.tensor_tensor(hid[:, k % 2, :], prod[:, k % 2, :], C[k % 2][:],
                                                ALU.mult).then_inc(s["hidden"], 1)

                    gated(0)
                    dve.wait_ge(s["pos"], b + 1)
                    steps.link(nc.vector.scalar_tensor_tensor(big(6), logits, float(CAPACITY), big(5),
                                                              ALU.is_lt, ALU.mult))
                    steps.link(nc.vector.tensor_reduce(tile_n[:], mask_b[:].rearrange("p t e -> p e t"),
                                                       AX.X, ALU.add))
                    steps.link(nc.vector.tensor_tensor(count[:], count[:], tile_n[:], ALU.add))
                    steps.link(nc.vector.tensor_copy(count_b[:], count[:]))
                    steps.link(nc.vector.tensor_copy(comb3[:, :, 0, :], big(6)))
                    steps.link(nc.vector.tensor_tensor(big(7), big(6), comb3[:, :, 0, :], ALU.subtract))
                    steps.link(nc.vector.tensor_copy(comb3[:, :, 1, :], big(7)))
                    nc.vector.tensor_tensor(comb3[:, :, 2, :], big(7), comb3[:, :, 1, :],
                                            ALU.subtract).then_inc(s["comb_parts"], 1)
                    gated(1)
                    dve.wait_ge(s["comb_ps"], b + 1)
                    nc.vector.tensor_copy(comb_t[0:SPLIT3 * E, :], M_comb).then_inc(s["comb_ready"], 1)
                    for k in range(2, GROUPS):
                        gated(k)
                        if k - 1 >= NSH:
                            weighted(k - 1)
                        if k == 6:
                            nxt = (b + 1) & (B - 1)
                            if tag == "f1":
                                dve.wait_ge(in_x, 16 * B)
                            layer_norm(dve, steps, x_tile(nxt)).then_inc(s["xn_ready"], 1)
                    weighted(GROUPS - 1)
                    dve.wait_ge(s["x_hi_ready"], b + 2)
                    nc.vector.tensor_tensor(x_lo[:], M[:], x_hi[:], ALU.subtract).then_inc(s["x_lo_ready"], 1)
                    dve.wait_ge(s["yt_ps"], b + 1)
                    xb = x_tok[:, bass.ds(b, 1), :, :].rearrange("p a t d -> p (a t d)")
                    nc.vector.tensor_tensor(xb, M[:], xb, ALU.add).then_inc(s["x_done"], 1)
                    dve.wait_ge(s["x_done"], b + 1)
                    assert steps.n == per, (steps.n, per)

            def sync(sp):
                if last:
                    with sp.Fori(0, B) as b:
                        sp.wait_ge(s["x_done"], b + 1)
                        sp.dma_start(out[bass.ds(b, 1)].rearrange("a (t p) d -> p (a t) d", p=P),
                                     x_tok[:, bass.ds(b, 1)].rearrange("p a t d -> p (a t) d")).then_inc(stored, 16)
                    sp.wait_ge(stored, 16 * B)
            return dict(tensor=pe, scalar=act, vector=dve, sync=sync)

        def attention():
            s = {n: sem(f"att_{n}") for n in (
                "xn_ready", "xt_ps", "x_hi_ready", "x_lo_ready", "qk_ps", "roped", "qk_ready", "v_ps", "v_ready",
                "scores", "maxes", "probs", "pt_ps", "pt_by_dve", "pt_by_act", "o_ps", "rec_ready", "rec_ps",
                "rec_copied", "o_ready", "y_ps", "y_copied", "yt_ps", "x_done")}
            S, PT = (bank[0], bank[1]), (bank[2], bank[3])
            O, R, J, Y = bank[4], bank[5], bank[6], bank[7]
            step_sem, pool_step = dve_step["att"], sem("pool_step")
            LN = LN_STEPS
            REC = 4
            VG = 2 * TT

            def transposed_at(j, u):
                if u >= LAG:
                    return j, u - LAG
                return (j - 1, u - LAG + UNITS) if j > 0 else None

            def moved(b, j, u, on_dve):
                mine = [v for v in range(UNITS) if (v in EVAC_ON_DVE) == on_dve]
                return b * (PAIRS * len(mine)) + j * len(mine) + sum(v <= u for v in mine)

            def pe(pe):
                j_read = {}

                def free_j():
                    if j_read:
                        pe.wait_ge(j_read["sem"], j_read["at"])

                def front(b):
                    pe.wait_ge(s["xn_ready"], b + 1)
                    free_j()
                    for t in range(TT):
                        ins = nc.tensor.transpose(J[:, t * P:(t + 1) * P], xn[:, t, :], ident[:])
                    ins.then_inc(s["xt_ps"], 1)
                    j_read.update(sem=s["x_lo_ready"], at=b + 1)

                def project(b, j, part):
                    if (j, part) == (0, 0):
                        pe.wait_ge(s["x_hi_ready"], b + 1)
                    free_j()
                    for n, (w, a) in enumerate(((qk_hi, x_hi), (qk_lo, x_hi), (qk_hi, x_lo))):
                        ins = nc.tensor.matmul(J[:], w[:, j, part, :], a[:], start=(n == 0), stop=(n == 2))
                    ins.then_inc(s["qk_ps"], 1)
                    j_read.update(sem=s["roped"], at=b * (PAIRS * PARTS) + (j * PARTS + part + 1))

                def values(b, i):
                    t, half = divmod(i, 2)
                    free_j()
                    cols = slice(half * T, (half + 1) * T)
                    tok = slice(t * P, (t + 1) * P)
                    for n, (a, w) in enumerate(((x_hi, v_hi), (x_lo, v_hi), (x_hi, v_lo))):
                        ins = nc.tensor.matmul(J[:], a[:, tok], w[:, cols], start=(n == 0), stop=(n == 2))
                    ins.then_inc(s["v_ps"], 1)
                    j_read.update(sem=s["v_ready"], at=b * VG + (i + 1))

                def scores(b, j, u):
                    n = b * (PAIRS * UNITS) + (j * UNITS + u)
                    h, qt = divmod(u, TT)
                    if u == 0:
                        pe.wait_ge(s["qk_ready"], b * PAIRS + (j + 1))
                    if j or u >= 2:
                        pe.wait_ge(s["probs"], n - 1)
                    nc.tensor.matmul(S[u % 2][:], q_pad[:, j % 2, h, qt * P:(qt + 1) * P], k_rot[:, j % 2, :],
                                     start=True, stop=True).then_inc(s["scores"], 1)

                def transposes(b, j, u):
                    n = b * (PAIRS * UNITS) + (j * UNITS + u)
                    pe.wait_ge(s["probs"], n + 1)
                    if j or u >= 2:
                        pj, pu = (j, u - 2) if u >= 2 else (j - 1, u - 2 + UNITS)
                        by_dve = pu in EVAC_ON_DVE
                        pe.wait_ge(s["pt_by_dve" if by_dve else "pt_by_act"], moved(b, pj, pu, by_dve))
                    for k in range(TT):
                        ins = nc.tensor.transpose(PT[u % 2][:, k * P:(k + 1) * P],
                                                  prob[:, u % NP, k * P:(k + 1) * P], ident[:])
                    ins.then_inc(s["pt_ps"], 1)

                def apply_v(b, j):
                    for by_dve in (True, False):
                        pe.wait_ge(s["pt_by_dve" if by_dve else "pt_by_act"], moved(b, j, UNITS - 1, by_dve))
                    if j:
                        pe.wait_ge(s["o_ready"], b * PAIRS + j)
                    if j == 0:
                        pe.wait_ge(s["v_ready"], b * VG + VG)
                    for k in range(TT):
                        for h in range(2):
                            head = slice((2 * j + h) * DH, (2 * j + h + 1) * DH)
                            ins = nc.tensor.matmul(O[h * DH:(h + 1) * DH, :], v_all[:, k, head],
                                                   pt[:, j % 2, h, k, :], start=(k == 0), stop=(k == TT - 1))
                    ins.then_inc(s["o_ps"], 1)

                def reciprocals(b, j):
                    pe.wait_ge(s["rec_ready"], b * PAIRS + (j + 1))
                    if j:
                        pe.wait_ge(s["rec_copied"], b * PAIRS + j)
                    for qt in range(TT):
                        for a in range(SPLIT3):
                            for h in range(2):
                                ins = nc.tensor.matmul(
                                    R[h * DH:(h + 1) * DH, qt * P:(qt + 1) * P],
                                    rec3[:, j % 2, a, h, qt:qt + 1].broadcast_to([P, DH]),
                                    ident_b[:], start=(a == 0), stop=(a == SPLIT3 - 1))
                    ins.then_inc(s["rec_ps"], 1)

                def project_out(b, j):
                    pe.wait_ge(s["o_ready"], b * PAIRS + (j + 1))
                    nc.tensor.matmul(Y[:], wo[:, j, :], o_t[:, j % 2, :], start=(j == 0),
                                     stop=(j == PAIRS - 1)).then_inc(s["y_ps"], 1)

                pe.wait_ge(w_lo_ready, 4)
                front(0)
                for part in range(PARTS):
                    project(0, 0, part)
                for i in range(VG):
                    values(0, i)
                with pe.Fori(0, B) as b:
                    j_read.update(sem=s["v_ready"], at=b * VG + VG)
                    for j in range(PAIRS):
                        for u in range(UNITS):
                            scores(b, j, u)
                            if u % 2 == 0 and j < PAIRS - 1:
                                project(b, j + 1, u // 2)
                            if (j, u) == (PAIRS - 1, 1):
                                front(b + 1)
                            if at := transposed_at(j, u):
                                transposes(b, *at)
                            if j and u == 3:
                                apply_v(b, j - 1)
                            if j and u == 4:
                                reciprocals(b, j - 1)
                            if j and u == 6:
                                project_out(b, j - 1)
                    j = PAIRS - 1
                    for part, u in enumerate(range(UNITS - LAG, UNITS)):
                        transposes(b, j, u)
                        project(b + 1, 0, part)
                    project(b + 1, 0, PARTS - 1)
                    apply_v(b, j)
                    for i in range(VG):
                        values(b + 1, i)
                        if i == 1:
                            reciprocals(b, j)
                        if i == 3:
                            project_out(b, j)
                        if i == 5:
                            pe.wait_ge(s["y_copied"], b + 1)
                            free_j()
                            for t in range(TT):
                                ins = nc.tensor.transpose(J[:, t * P:(t + 1) * P], y_t[:, t * P:(t + 1) * P], ident[:])
                            ins.then_inc(s["yt_ps"], 1)
                            j_read.update(sem=s["x_done"], at=b + 1)

            def act(act):
                def x_high(b):
                    act.wait_ge(s["xt_ps"], b + 1)
                    nc.scalar.activation(x_hi[:], J[:], ACT.Copy).then_inc(s["x_hi_ready"], 1)

                def values(b, i):
                    t, half = divmod(i, 2)
                    act.wait_ge(s["v_ps"], b * VG + (i + 1))
                    nc.scalar.activation(v_all[:, t, half * T:(half + 1) * T], J[:], ACT.Copy)\
                      .then_inc(s["v_ready"], 1)

                def exponentials(b, j, u):
                    n = b * (PAIRS * UNITS) + (j * UNITS + u)
                    act.wait_ge(s["maxes"], n + 1)
                    if j or u >= NP:
                        act.wait_ge(s["pt_ps"], n - (NP - 1))
                    nc.scalar.activation(prob[:, u % NP, :], S[u % 2][:], ACT.Exp,
                                         bias=neg_max[:, j % 2, u:u + 1],
                                         accum_out=den[:, j % 2, u:u + 1]).then_inc(s["probs"], 1)

                def move(b, j, u):
                    if u in EVAC_ON_DVE:
                        return
                    h, qt = divmod(u, TT)
                    act.wait_ge(s["pt_ps"], b * (PAIRS * UNITS) + (j * UNITS + u + 1))
                    nc.scalar.activation(pt[:, j % 2, h, :, qt * P:(qt + 1) * P],
                                         PT[u % 2][:].rearrange("p (k q) -> p k q", q=P),
                                         ACT.Copy).then_inc(s["pt_by_act"], 1)

                def copy_reciprocals(b, j):
                    act.wait_ge(s["rec_ps"], b * PAIRS + (j + 1))
                    if j:
                        act.wait_ge(s["o_ready"], b * PAIRS + j)
                    nc.scalar.activation(rec_all[:], R[:], ACT.Copy).then_inc(s["rec_copied"], 1)

                x_high(0)
                act.wait_ge(w_lo_ready, 4)
                for i in range(VG):
                    values(0, i)
                with act.Fori(0, B) as b:
                    for j in range(PAIRS):
                        for u in range(UNITS):
                            exponentials(b, j, u)
                            if (j, u) == (PAIRS - 1, 1):
                                x_high(b + 1)
                            if at := transposed_at(j, u):
                                move(b, *at)
                            if j and u == 4:
                                copy_reciprocals(b, j - 1)
                    j = PAIRS - 1
                    for u in range(UNITS - LAG, UNITS):
                        move(b, j, u)
                    act.wait_ge(s["o_ps"], (b + 1) * PAIRS)
                    for i in range(VG):
                        values(b + 1, i)
                        if i == 1:
                            copy_reciprocals(b, j)
                        if i == 3:
                            act.wait_ge(s["y_ps"], (b + 1) * PAIRS)
                            nc.scalar.activation(y_t[:], Y[:], ACT.Identity, bias=bo[:, 0:1]).then_inc(s["y_copied"], 1)

            def dve(dve):
                def x_low(b):
                    dve.wait_ge(s["x_hi_ready"], b + 1)
                    nc.vector.tensor_tensor(x_lo[:], J[:], x_hi[:], ALU.subtract).then_inc(s["x_lo_ready"], 1)

                def rope_part(b, j, part):
                    dve.wait_ge(s["qk_ps"], b * (PAIRS * PARTS) + (j * PARTS + part + 1))
                    nc.vector.tensor_tensor(rope_tmp[:, j % 2, part, :], J[:], rope_t[:, part, :],
                                            ALU.mult).then_inc(s["roped"], 1)

                def maxima(b, j, u):
                    dve.wait_ge(s["scores"], b * (PAIRS * UNITS) + (j * UNITS + u + 1))
                    nc.vector.tensor_reduce(neg_max[:, j % 2, u:u + 1], S[u % 2][:], AX.X, ALU.max,
                                            negate=True).then_inc(s["maxes"], 1)

                def move(b, j, u):
                    if u not in EVAC_ON_DVE:
                        return
                    h, qt = divmod(u, TT)
                    dve.wait_ge(s["pt_ps"], b * (PAIRS * UNITS) + (j * UNITS + u + 1))
                    nc.vector.tensor_copy(pt[:, j % 2, h, :, qt * P:(qt + 1) * P],
                                          PT[u % 2][:].rearrange("p (k q) -> p k q", q=P)).then_inc(s["pt_by_dve"], 1)

                def reciprocals(b, j):
                    dve.wait_ge(s["probs"], b * (PAIRS * UNITS) + (j + 1) * UNITS)
                    parts = [rec3[:, j % 2, a].rearrange("p h t -> p (h t)") for a in range(SPLIT3)]
                    steps.link(nc.vector.reciprocal(rec[:, 0, :], den[:, j % 2, :]))
                    steps.link(nc.vector.tensor_copy(parts[0], rec[:, 0, :]))
                    steps.link(nc.vector.tensor_tensor(rec[:, 1, :], rec[:, 0, :], parts[0], ALU.subtract))
                    steps.link(nc.vector.tensor_copy(parts[1], rec[:, 1, :]))
                    nc.vector.tensor_tensor(parts[2], rec[:, 1, :], parts[1], ALU.subtract).then_inc(s["rec_ready"], 1)

                def normalise(b, j):
                    dve.wait_ge(s["o_ps"], b * PAIRS + (j + 1))
                    dve.wait_ge(s["rec_copied"], b * PAIRS + (j + 1))
                    nc.vector.tensor_tensor(o_t[:, j % 2, :], O[:], rec_all[:], ALU.mult).then_inc(s["o_ready"], 1)

                steps = Steps(dve, step_sem)
                layer_norm(dve, steps, lambda t: x_tok[:, 0, t, :]).then_inc(s["xn_ready"], 1)
                x_low(0)
                dve.wait_ge(w_lo_ready, 4)
                for part in range(PARTS):
                    rope_part(0, 0, part)
                first, per = steps.n, LN + REC * PAIRS
                with dve.Fori(0, B) as b:
                    steps = Steps(dve, step_sem, b * per + first)
                    for j in range(PAIRS):
                        for u in range(UNITS):
                            maxima(b, j, u)
                            if u % 2 == 0 and j < PAIRS - 1:
                                rope_part(b, j + 1, u // 2)
                            if (j, u) == (PAIRS - 1, 1):
                                x_low(b + 1)
                            if at := transposed_at(j, u):
                                move(b, *at)
                            if j and u == 2:
                                reciprocals(b, j - 1)
                            if j and u == 5:
                                normalise(b, j - 1)
                            if (j, u) == (4, 7):
                                nxt = (b + 1) & (B - 1)
                                layer_norm(dve, steps, x_tile(nxt)).then_inc(s["xn_ready"], 1)
                    j = PAIRS - 1
                    move(b, j, UNITS - 3)
                    rope_part(b + 1, 0, 0)
                    move(b, j, UNITS - 2)
                    rope_part(b + 1, 0, 1)
                    move(b, j, UNITS - 1)
                    rope_part(b + 1, 0, 2)
                    reciprocals(b, j)
                    rope_part(b + 1, 0, 3)
                    normalise(b, j)
                    dve.wait_ge(s["yt_ps"], b + 1)
                    xb = x_tok[:, bass.ds(b, 1), :, :].rearrange("p a t d -> p (a t d)")
                    nc.vector.tensor_tensor(xb, J[:], xb, ALU.add).then_inc(s["x_done"], 1)
                    dve.wait_ge(s["x_done"], b + 1)
                    assert steps.n == per, (steps.n, per)

            def pool(pool):
                def rotate(b, j):
                    g = b * PAIRS + j
                    tmp = lambda part: rope_tmp[:, j % 2, part, :]
                    steps = Steps(pool, pool_step, g * 4)
                    pool.wait_ge(s["roped"], g * PARTS + 2)
                    steps.link(nc.gpsimd.tensor_tensor(tmp(0), tmp(0), fenc[:, 0, :], ALU.add))
                    for h in range(2):
                        rows = slice(h * DH, (h + 1) * DH)
                        steps.link(nc.gpsimd.tensor_tensor(q_pad[rows, j % 2, h, :], tmp(0)[rows], tmp(1)[rows], ALU.add))
                    pool.wait_ge(s["roped"], g * PARTS + PARTS)
                    steps.link(nc.gpsimd.tensor_tensor(tmp(2), tmp(2), fenc[:, 1, :], ALU.add))
                    nc.gpsimd.tensor_tensor(k_rot[:, j % 2, :], tmp(2), tmp(3), ALU.add).then_inc(s["qk_ready"], 1)
                    assert steps.n == 4

                pool.wait_ge(fenc_ready, 2)
                pool.wait_ge(consts_ready, 3)
                rotate(0, 0)
                with pool.Fori(0, B) as b:
                    for j in range(1, PAIRS):
                        rotate(b, j)
                    rotate(b + 1, 0)
            return dict(tensor=pe, scalar=act, vector=dve, gpsimd=pool)

        def x_tile(b):
            return lambda t: x_tok[:, bass.ds(b, 1), t, :].rearrange("p a d -> p (a d)")

        ffn1, att, ffn2 = ffn("f1", False), attention(), ffn("f2", True)

        @block.sync
        def _(sp):
            setup_sync(sp)
            ffn2["sync"](sp)

        @block.scalar
        def _(act):
            setup_act(act)
            ffn1["scalar"](act)
            att["scalar"](act)
            ffn2["scalar"](act)

        @block.vector
        def _(dve):
            setup_dve(dve)
            ffn1["vector"](dve)
            att["vector"](dve)
            ffn2["vector"](dve)

        @block.tensor
        def _(pe):
            setup_pe(pe)
            ffn1["tensor"](pe)
            att["tensor"](pe)
            ffn2["tensor"](pe)

        @block.gpsimd
        def _(pool):
            setup_pool(pool)
            att["gpsimd"](pool)


def kernel(L0_attn_x, L0_attn_w_qkv, L0_attn_w_fproj, L0_attn_b_fproj, L0_attn_w_out, L0_attn_b_out,
           L0_ffn_gate_w, L0_ffn_we_gate, L0_ffn_we_up, L0_ffn_we_down, L0_ffn_ws_gate, L0_ffn_ws_up,
           L0_ffn_ws_down):
    import ml_dtypes
    import numpy as np
    import concourse.bacc as bacc
    from concourse.bass_utils import run_bass_kernel_spmd

    a = np.asarray
    wqkv = a(L0_attn_w_qkv).reshape(3, HEADS, DH, D)
    half = DH // 2
    turned = np.r_[2 * np.arange(half) + 1, 2 * np.arange(half)]
    qk = np.stack([wqkv[0], wqkv[0][:, turned], wqkv[1], wqkv[1][:, turned]])
    qk = qk.reshape(PARTS, PAIRS, P, D).transpose(3, 1, 0, 2)
    gate = np.concatenate([a(L0_ffn_ws_gate).reshape(NSH, P, D), a(L0_ffn_we_gate)])
    up = np.concatenate([a(L0_ffn_ws_up).reshape(NSH, P, D), a(L0_ffn_we_up)])
    ws_down = a(L0_ffn_ws_down).reshape(D, NSH, P).transpose(2, 1, 0)
    we_down = a(L0_ffn_we_down).transpose(2, 0, 1)
    fproj = a(L0_attn_w_fproj).T

    freqs = np.float32(10000.0) ** (-np.arange(0, DH, 2, dtype=np.float32) / np.float32(DH))
    pos = np.arange(T, dtype=np.float32)
    angles = (pos[:, None] * freqs[None, :]).astype(np.float32).astype(np.float64)
    cos = np.repeat(np.cos(angles), 2, axis=1).T
    sin = np.repeat(np.sin(angles), 2, axis=1).T * np.where(np.arange(DH) < half, -1.0, 1.0)[:, None]
    rope = np.stack([cos * QSCALE, sin * QSCALE, cos, sin]).astype(np.float32)
    rope = np.concatenate([rope, rope], axis=1).transpose(1, 0, 2)
    nf = np.arange(1, NF // 2 + 1, dtype=np.float32)
    fa = (nf[:, None] * pos[None, :]).astype(np.float64)
    fourier = np.concatenate([np.sin(fa), np.cos(fa)]).astype(np.float32)
    ident = np.eye(P, dtype=np.float32)
    lower = np.zeros((P, P), np.float32)
    lower[:, :E * E] = (np.arange(E)[None, :] < np.arange(E)[:, None]).reshape(-1)
    before = np.triu(np.ones((P, P), np.float32), 1)
    sel = np.zeros((P, E, P), np.float32)
    for r in range(SPLIT3 * E):
        sel[r, r % E] = 1.0

    bf = ml_dtypes.bfloat16
    arrays = {
        "x": a(L0_attn_x),
        "w_gate_up": np.concatenate([gate, up]).transpose(2, 0, 1).reshape(P, -1),
        "w_down": np.concatenate([ws_down, we_down], axis=1).reshape(P, -1),
        "gate_t": a(L0_ffn_gate_w).T,
        "w_qk": qk.reshape(P, -1),
        "w_v": wqkv[2].reshape(INNER, D).T,
        "w_out": a(L0_attn_w_out).reshape(D, PAIRS, P).transpose(2, 1, 0).reshape(P, -1),
        "b_out": a(L0_attn_b_out)[:, None],
        "fproj": np.concatenate([fproj, fproj], axis=1),
        "bproj": np.concatenate([a(L0_attn_b_fproj)] * 2)[:, None],
        "rope": rope.reshape(P, -1),
        "fourier": fourier,
        "consts": np.stack([ident, lower]),
        "consts_b": np.stack([before, ident]).astype(bf),
        "sel": sel.reshape(P, -1).astype(bf),
    }
    nc = bacc.Bacc("TRN2", target_bir_lowering=False, num_devices=1)
    inputs, args = {}, []
    for name, v in arrays.items():
        v = np.ascontiguousarray(v)
        inputs[f"in_{name}"] = v
        args.append(nc.dram_tensor(f"in_{name}", v.shape, mybir.dt.from_np(v.dtype), kind="ExternalInput").ap())
    out = nc.dram_tensor("out", (B, T, D), F32, kind="ExternalOutput").ap()
    macaron(nc, *args, out)
    r = run_bass_kernel_spmd(nc, [inputs], core_ids=[0])
    return r.results[0]["out"]
```

```python
from contextlib import ExitStack

import concourse.bass as bass
from concourse import mybir

F32 = mybir.dt.float32
F32R = mybir.dt.float32r
BF16 = mybir.dt.bfloat16
I32 = mybir.dt.int32
ALU = mybir.AluOpType
ACT = mybir.ActivationFunctionType
AX = mybir.AxisListType

P = 128
B, T, D = 8, 512, 128
TT = T // P
HEADS, DH = 16, 64
INNER = HEADS * DH
PAIRS = HEADS // 2
NF = 32
E, NSH, TOPK = 8, 2, 2
GROUPS = NSH + E
CAPACITY = -(-5 * B * T * TOPK // (4 * E))
EPS = 1e-5
QSCALE = DH ** -0.5
UNITS = 2 * TT
PARTS = 4
LAG = 3
NP = 4
SPLIT3 = 3
RSQRT_MAGIC = 0x5F3759DF
NEWTON = 3
LN_STAGES = 7 + 3 * NEWTON
LN_STEPS = TT + 7 + 2 + 4 * NEWTON + TT - 1


class Steps:

    def __init__(self, eng, sem, base=0):
        self.eng, self.sem, self.base, self.n = eng, sem, base, 0

    def mark(self, ins):
        ins.then_inc(self.sem, 1)
        self.n += 1

    def wait(self):
        self.eng.wait_ge(self.sem, self.base + self.n)

    def link(self, ins):
        self.mark(ins)
        self.wait()


def macaron(nc, x, w_gate_up, w_down, gate_t, w_qk, w_v, w_out, b_out, fproj, bproj,
            rope, fourier, consts, consts_b, sel, out):
    with ExitStack() as ctx:
        def sb(name, shape, dt=F32):
            return ctx.enter_context(nc.sbuf_tensor(name, shape, dt))

        def sem(name):
            return ctx.enter_context(nc.semaphore(name))

        x_tok = sb("x_tok", [P, B, TT, D])
        gu_hi = sb("gu_hi", [P, 2 * GROUPS, P], F32R)
        gu_lo = sb("gu_lo", [P, 2 * GROUPS, P], F32R)
        down_hi = sb("down_hi", [P, GROUPS, D], F32R)
        down_lo = sb("down_lo", [P, GROUPS, D], F32R)
        gate_w = sb("gate_w", [P, E])
        gate_hi = sb("gate_hi", [P, E], F32R)
        gate_lo = sb("gate_lo", [P, E], F32R)
        qk_hi = sb("qk_hi", [P, PAIRS, PARTS, P], F32R)
        qk_lo = sb("qk_lo", [P, PAIRS, PARTS, P], F32R)
        v_hi = sb("v_hi", [P, INNER], F32R)
        v_lo = sb("v_lo", [P, INNER], F32R)
        wo = sb("wo", [P, PAIRS, D])
        bo = sb("bo", [P, 1])
        rope_t = sb("rope_t", [P, 2, T])
        fenc = sb("fenc", [P, 2, T])
        ident = sb("ident", [P, P])
        ident_b = sb("ident_b", [P, P], BF16)
        before_b = sb("before_b", [P, P], BF16)
        ones_b = sb("ones_b", [P, P], BF16)
        lower = sb("lower", [P, E, E])
        sel_b = sb("sel_b", [P, E, P], BF16)
        x_hi = sb("x_hi", [P, T], F32R)
        x_lo = sb("x_lo", [P, T], F32R)
        xn = sb("xn", [P, TT, D])
        y_t = xn[:].rearrange("p t d -> p (t d)")
        stats = sb("stats", [P, TT, 6])
        mv = sb("mv", [P, TT, 2])
        mean = sb("mean", [P, TT])
        ve = sb("ve", [P, TT])
        rs = sb("rs", [P, TT])
        rsi = sb("rsi", [P, TT], I32)
        nt = sb("nt", [P, 3, TT])
        work = sb("work", [P, 3 * 4096])
        v_all = work[:, 0:4096].rearrange("p (t n) -> p t n", t=TT)
        pt = work[:, 4096:].rearrange("p (g h k q) -> p g h k q", g=2, h=2, k=TT)
        st_qk = work[:, 0:PAIRS * PARTS * P].rearrange("p (a b n) -> p a b n", a=PAIRS, b=PARTS)
        st_v = work[:, 4096:4096 + INNER]
        st_gu = work[:, 4096 + INNER:4096 + INNER + 2 * GROUPS * P]
        prob = sb("prob", [P, NP, T])
        act_g, prod = prob[:, 0:2, :], prob[:, 2:4, :]
        hid = sb("hid", [P, 2, T])
        o_t = hid
        comb_t = sb("comb_t", [P, T], BF16)
        route = sb("route", [P, 8, TT, E])
        pair_gt = sb("pair_gt", [P, TT, E, E])
        pair_ge = sb("pair_ge", [P, TT, E, E])
        small = sb("small", [P, 8, TT])
        mask_b = sb("mask_b", [P, TT, E], BF16)
        count_b = sb("count_b", [P, E], BF16)
        count = sb("count", [P, E])
        tile_n = sb("tile_n", [P, E])
        comb3 = sb("comb3", [P, TT, SPLIT3, E], BF16)
        q_st = sb("q_st", [P, 2, 2, T], F32R)
        k_hh = sb("k_hh", [P, 2, 2, T], F32R)
        k_ll = sb("k_ll", [P, 2, 2, T], F32R)
        hid_hi, hid_lo = k_hh[:, 0], k_ll[:, 0]
        rope_tmp = sb("rope_tmp", [P, PARTS, T])
        neg_max = sb("neg_max", [P, 2, UNITS])
        den = sb("den", [P, 2, UNITS])
        rec = sb("rec", [P, 3, UNITS])
        rec3 = sb("rec3", [P, 2, SPLIT3, 2, TT], BF16)
        rec_all = sb("rec_all", [P, T])
        st_down = work[:, 4096 + INNER + 2 * GROUPS * P:4096 + INNER + 3 * GROUPS * P]
        free = 4096 + INNER + 3 * GROUPS * P
        fourier_s, fproj_s = work[0:NF, free:free + T], work[0:NF, free + T:free + T + P]
        bproj_s = sb("bproj_s", [P, 1])

        bank = [ctx.enter_context(nc.psum_tensor(f"bank{i}", [P, T], F32)) for i in range(8)]

        in_x, in_ffn, in_att, in_small = sem("in_x"), sem("in_ffn"), sem("in_att"), sem("in_small")
        consts_ready = sem("consts_ready")
        w_hi_ready, w_lo_ready = sem("w_hi_ready"), sem("w_lo_ready")
        fenc_ps, fenc_ready = sem("fenc_ps"), sem("fenc_ready")
        dve_step = {ph: sem(f"dve_step_{ph}") for ph in ("setup", "f1", "att", "f2")}
        stored = sem("stored")
        q_split = sem("q_split")
        k_own_low = sem("k_own_low")
        k_far_high = sem("k_far_high")

        block = ctx.enter_context(nc.Block())
        progs = {e: [] for e in ("sync", "scalar", "vector", "tensor", "gpsimd")}

        def setup_sync(sp):
            sp.dma_start(x_tok[:, 0], x[0].rearrange("(t p) d -> p t d", p=P)).then_inc(in_x, 16)
            sp.dma_start(gate_w[:], gate_t).then_inc(in_small, 16)
            sp.dma_start(ident[:], consts[0]).then_inc(in_small, 16)
            sp.dma_start(st_gu, w_gate_up).then_inc(in_ffn, 16)
            sp.dma_start(st_down, w_down).then_inc(in_ffn, 16)
            for b in range(1, B):
                sp.dma_start(x_tok[:, b], x[b].rearrange("(t p) d -> p t d", p=P)).then_inc(in_x, 16)
            sp.dma_start(work[:, 0:PAIRS * PARTS * P], w_qk).then_inc(in_att, 16)
            sp.dma_start(st_v, w_v).then_inc(in_att, 16)
            sp.dma_start(wo[:].rearrange("p g d -> p (g d)"), w_out).then_inc(in_att, 16)

        def setup_act(act):
            act.dma_start(before_b[:], consts_b[0]).then_inc(in_small, 16)
            act.dma_start(ident_b[:], consts_b[1]).then_inc(in_small, 16)
            act.dma_start(sel_b[:].rearrange("p e m -> p (e m)"), sel).then_inc(in_small, 16)
            act.dma_start(lower[:].rearrange("p a b -> p (a b)"), consts[1][:, 0:E * E]).then_inc(in_small, 16)
            act.dma_start(rope_t[:].rearrange("p a t -> p (a t)"), rope).then_inc(in_small, 16)
            act.dma_start(fourier_s, fourier).then_inc(in_small, 16)
            act.dma_start(fproj_s, fproj).then_inc(in_small, 16)
            act.dma_start(bproj_s[:], bproj).then_inc(in_small, 16)
            act.dma_start(bo[:], b_out).then_inc(in_small, 16)
            act.wait_ge(in_small, 11 * 16)
            nc.scalar.activation(gate_hi[:], gate_w[:], ACT.Copy).then_inc(w_hi_ready, 1)
            act.wait_ge(in_ffn, 32)
            nc.scalar.activation(gu_hi[:].rearrange("p g n -> p (g n)"), st_gu, ACT.Copy).then_inc(w_hi_ready, 1)
            nc.scalar.activation(down_hi[:].rearrange("p g n -> p (g n)"), st_down, ACT.Copy).then_inc(w_hi_ready, 1)
            act.wait_ge(in_att, 48)
            nc.scalar.activation(qk_hi[:, :, 2:4], st_qk[:, :, 2:4], ACT.Copy)
            nc.scalar.activation(qk_hi[:, :, 0:2], st_qk[:, :, 0:2], ACT.Copy, scale=QSCALE).then_inc(w_hi_ready, 1)
            nc.scalar.activation(v_hi[:], st_v, ACT.Copy).then_inc(w_hi_ready, 1)
            act.wait_ge(fenc_ps, 1)
            nc.scalar.activation(fenc[:, 1, :], bank[7][:], ACT.Identity, bias=bproj_s[:, 0:1]).then_inc(fenc_ready, 1)
            act.wait_ge(fenc_ready, 1)
            nc.scalar.activation(fenc[:, 0, :], fenc[:, 1, :], ACT.Copy, scale=QSCALE).then_inc(fenc_ready, 1)

        def setup_dve(dve):
            nc.vector.memset(ones_b[:], 1.0).then_inc(consts_ready, 1)
            nc.vector.memset(comb_t[:], 0.0).then_inc(consts_ready, 1)
            dve.wait_ge(w_hi_ready, 1)
            nc.vector.tensor_tensor(gate_lo[:], gate_w[:], gate_hi[:], ALU.subtract).then_inc(w_lo_ready, 1)
            dve.wait_ge(w_hi_ready, 2)
            nc.vector.tensor_tensor(gu_lo[:].rearrange("p g n -> p (g n)"), st_gu,
                                    gu_hi[:].rearrange("p g n -> p (g n)"), ALU.subtract).then_inc(w_lo_ready, 1)
            dve.wait_ge(w_hi_ready, 3)
            nc.vector.tensor_tensor(down_lo[:].rearrange("p g n -> p (g n)"), st_down,
                                    down_hi[:].rearrange("p g n -> p (g n)"), ALU.subtract).then_inc(w_lo_ready, 1)
            dve.wait_ge(w_hi_ready, 5)
            nc.vector.tensor_tensor(qk_lo[:, :, 2:4], st_qk[:, :, 2:4], qk_hi[:, :, 2:4], ALU.subtract)
            nc.vector.scalar_tensor_tensor(qk_lo[:, :, 0:2], st_qk[:, :, 0:2], QSCALE, qk_hi[:, :, 0:2],
                                           ALU.mult, ALU.subtract).then_inc(w_lo_ready, 1)
            nc.vector.tensor_tensor(v_lo[:], st_v, v_hi[:], ALU.subtract).then_inc(w_lo_ready, 1)

        def setup_pe(pe):
            pe.wait_ge(in_small, 11 * 16)
            nc.tensor.matmul(bank[7][:], fproj_s, fourier_s, start=True, stop=True).then_inc(fenc_ps, 1)

        def norm_stage(steps, n, xb):
            even, odd = stats[:, :, 0:3], stats[:, :, 3:6]
            steps.wait()
            if n == 0:
                for t in range(TT):
                    steps.mark(nc.vector.bn_stats(stats[:, t, :], xb(t)))
            elif n == 1:
                steps.mark(nc.vector.tensor_tensor(mv[:, :, 0], even[:, :, 1], odd[:, :, 1], ALU.add))
                steps.mark(nc.vector.tensor_tensor(mv[:, :, 1], even[:, :, 1], odd[:, :, 1], ALU.subtract))
                steps.mark(nc.vector.tensor_tensor(ve[:], even[:, :, 2], odd[:, :, 2], ALU.add))
            elif n == 2:
                steps.mark(nc.vector.tensor_scalar(mean[:], mv[:, :, 0], 0.5, None, ALU.mult))
                steps.mark(nc.vector.tensor_scalar(rs[:], ve[:], 1.0 / D, EPS, ALU.mult, ALU.add))
                steps.mark(nc.vector.tensor_tensor(nt[:, 0, :], mv[:, :, 1], mv[:, :, 1], ALU.mult))
            elif n == 3:
                steps.mark(nc.vector.scalar_tensor_tensor(ve[:], nt[:, 0, :], 0.25, rs[:], ALU.mult, ALU.add))
            elif n == 4:
                steps.mark(nc.vector.tensor_scalar(rsi[:], ve[:].bitcast(I32), 1, None, ALU.logical_shift_right))
            elif n == 5:
                steps.mark(nc.vector.tensor_scalar(rs[:].bitcast(I32), rsi[:], -1, RSQRT_MAGIC, ALU.mult, ALU.add))
            elif n < LN_STAGES - 1:
                if n % 3 == 0:
                    steps.mark(nc.vector.tensor_tensor(nt[:, 0, :], ve[:], rs[:], ALU.mult))
                    steps.mark(nc.vector.tensor_scalar(nt[:, 2, :], rs[:], -0.5, None, ALU.mult))
                elif n % 3 == 1:
                    steps.mark(nc.vector.tensor_tensor(nt[:, 1, :], nt[:, 0, :], rs[:], ALU.mult))
                else:
                    steps.mark(nc.vector.scalar_tensor_tensor(rs[:], nt[:, 1, :], -3.0, nt[:, 2, :],
                                                              ALU.add, ALU.mult))
            else:
                for t in range(TT):
                    last = nc.vector.tensor_scalar(xn[:, t, :], xb(t), mean[:, t:t + 1], rs[:, t:t + 1],
                                                   ALU.subtract, ALU.mult)
                    if t < TT - 1:
                        steps.mark(last)
                return last

        def layer_norm(steps, xb):
            for n in range(LN_STAGES):
                last = norm_stage(steps, n, xb)
            return last

        def ffn(tag, last):
            s = {n: sem(f"{tag}_{n}") for n in (
                "xn_ready", "xt_ps", "x_hi_ready", "x_lo_ready", "logits", "shifted", "exps", "masks", "pos",
                "comb_parts", "comb_ps", "comb_ready", "gu_ps", "silu", "gated", "weight_ps", "hidden",
                "hid_hi_ready", "hid_lo_ready", "y_ps", "y_copied", "yt_ps", "x_done")}
            G, U, C = (bank[0], bank[1]), (bank[2], bank[3]), (bank[4], bank[5])
            Y, M = bank[6], bank[7]
            YT = C[0]
            M_log = M[:, 0:TT * E]
            M_comb = M[0:SPLIT3 * E, 0:T // 2].bitcast(BF16)
            step_sem = dve_step[tag]
            ROUTE_STEPS = 21

            def pe(pe):
                def front(b):
                    pe.wait_ge(s["xn_ready"], b + 1)
                    for t in range(TT):
                        ins = nc.tensor.transpose(M[:, t * P:(t + 1) * P], xn[:, t, :], ident[:])
                    ins.then_inc(s["xt_ps"], 1)

                def gate(b):
                    pe.wait_ge(s["x_hi_ready"], b + 1)
                    pe.wait_ge(s["x_lo_ready"], b + 1)
                    for t in range(TT):
                        tok = slice(t * P, (t + 1) * P)
                        for n, (a, w) in enumerate(((x_hi, gate_hi), (x_lo, gate_hi), (x_hi, gate_lo))):
                            ins = nc.tensor.matmul(M[:, t * E:(t + 1) * E], a[:, tok], w[:],
                                                   start=(n == 0), stop=(n == 2))
                    ins.then_inc(s["logits"], 1)

                def gate_up(b, k):
                    if k >= 2:
                        pe.wait_ge(s["gated"], b * GROUPS + (k - 1))
                    for dst, j in ((G[k % 2], 0), (U[k % 2], GROUPS)):
                        for n, (w, a) in enumerate(((gu_hi, x_hi), (gu_lo, x_hi), (gu_hi, x_lo))):
                            ins = nc.tensor.matmul(dst[:], w[:, j + k, :], a[:], start=(n == 0), stop=(n == 2))
                    ins.then_inc(s["gu_ps"], 1)

                def positions(b):
                    pe.wait_ge(s["masks"], b + 1)
                    nc.tensor.matmul(M_log, before_b[:], mask_b[:].rearrange("p t e -> p (t e)"),
                                     start=True, stop=False)
                    nc.tensor.matmul(M_log.rearrange("p (t e) -> p t e", e=E), ones_b[:],
                                     count_b[:].unsqueeze(1).broadcast_to([P, TT, E]), start=False, stop=False)
                    for t in range(TT - 1):
                        ins = nc.tensor.matmul(
                            M[:, (t + 1) * E:TT * E].rearrange("p (t e) -> p t e", e=E), ones_b[:],
                            mask_b[:, t:t + 1, :].broadcast_to([P, TT - 1 - t, E]), start=False, stop=(t == TT - 2))
                    ins.then_inc(s["pos"], 1)

                def combine_t(b):
                    pe.wait_ge(s["comb_parts"], b + 1)
                    for t in range(TT):
                        ins = nc.tensor.transpose(M_comb[:, t * P:(t + 1) * P],
                                                  comb3[:, t, :, :].rearrange("p a e -> p (a e)"), ident_b[:])
                    ins.then_inc(s["comb_ps"], 1)

                def weights(b, k):
                    e = k - NSH
                    if e == 0:
                        pe.wait_ge(s["comb_ready"], b + 1)
                    if e >= 2:
                        pe.wait_ge(s["hidden"], b * E + (e - 1))
                    nc.tensor.matmul(C[k % 2][:], sel_b[:, e, :], comb_t[:],
                                     start=True, stop=True).then_inc(s["weight_ps"], 1)

                def project(b, k):
                    pe.wait_ge(s["hid_lo_ready"], b * GROUPS + (k + 1))
                    for n, (w, a) in enumerate(((down_hi, hid_hi), (down_lo, hid_hi), (down_hi, hid_lo))):
                        ins = nc.tensor.matmul(Y[:], w[:, k, :], a[:, k % 2, :], start=(k == 0 and n == 0),
                                               stop=(k == GROUPS - 1 and n == 2))
                    ins.then_inc(s["y_ps"], 1)

                if tag == "f1":
                    pe.wait_ge(fenc_ready, 1)
                    pe.wait_ge(consts_ready, 2)
                    pe.wait_ge(w_lo_ready, 3)
                front(0)
                gate(0)
                gate_up(0, 0)
                positions(0)
                gate_up(0, 1)
                combine_t(0)
                with pe.Fori(0, B) as b:
                    for k in range(2, GROUPS):
                        gate_up(b, k)
                        if k - 1 >= NSH:
                            weights(b, k - 1)
                        project(b, k - 2)
                    front(b + 1)
                    weights(b, GROUPS - 1)
                    project(b, GROUPS - 2)
                    gate(b + 1)
                    gate_up(b + 1, 0)
                    project(b, GROUPS - 1)
                    positions(b + 1)
                    gate_up(b + 1, 1)
                    pe.wait_ge(s["y_copied"], b + 1)
                    for t in range(TT):
                        ins = nc.tensor.transpose(YT[:, t * P:(t + 1) * P], y_t[:, t * P:(t + 1) * P], ident[:])
                    ins.then_inc(s["yt_ps"], 1)
                    combine_t(b + 1)

            def act(act):
                def x_high(b):
                    act.wait_ge(s["xt_ps"], b + 1)
                    nc.scalar.activation(x_hi[:], M[:], ACT.Copy).then_inc(s["x_hi_ready"], 1)

                def exponentials(b):
                    act.wait_ge(s["shifted"], b + 1)
                    nc.scalar.activation(route[:, 1], route[:, 0], ACT.Exp).then_inc(s["exps"], 1)

                def silu(b, k):
                    act.wait_ge(s["gu_ps"], b * GROUPS + (k + 1))
                    if k >= 2:
                        act.wait_ge(s["gated"], b * GROUPS + (k - 1))
                    nc.scalar.activation(act_g[:, k % 2, :], G[k % 2][:], ACT.Silu).then_inc(s["silu"], 1)

                def hidden_high(b, k):
                    if k < NSH:
                        act.wait_ge(s["gated"], b * GROUPS + (k + 1))
                    else:
                        act.wait_ge(s["hidden"], b * E + (k - NSH + 1))
                    if k >= 2:
                        act.wait_ge(s["y_ps"], b * GROUPS + (k - 1))
                    nc.scalar.activation(hid_hi[:, k % 2, :], hid[:, k % 2, :], ACT.Copy)\
                      .then_inc(s["hid_hi_ready"], 1)

                x_high(0)
                exponentials(0)
                silu(0, 0)
                silu(0, 1)
                if tag == "f2":
                    act.wait_ge(q_split, B * PAIRS)
                    act.wait_ge(k_own_low, B * PAIRS)
                    act.wait_ge(k_far_high, B * PAIRS)
                hidden_high(0, 0)
                with act.Fori(0, B) as b:
                    for k in range(2, GROUPS):
                        silu(b, k)
                        hidden_high(b, k - 1)
                    x_high(b + 1)
                    hidden_high(b, GROUPS - 1)
                    exponentials(b + 1)
                    silu(b + 1, 0)
                    act.wait_ge(s["y_ps"], (b + 1) * GROUPS)
                    nc.scalar.activation(y_t, Y[:], ACT.Copy, scale=0.5).then_inc(s["y_copied"], 1)
                    silu(b + 1, 1)
                    hidden_high(b + 1, 0)

            def dve(dve):
                big, small_t = (lambda n: route[:, n]), (lambda n: small[:, n, :])
                per_e = lambda ap: ap.unsqueeze(2).broadcast_to([P, TT, E])
                logits = M_log.rearrange("p (t e) -> p t e", e=E)

                def x_low(b):
                    dve.wait_ge(s["x_hi_ready"], b + 1)
                    nc.vector.tensor_tensor(x_lo[:], M[:], x_hi[:], ALU.subtract).then_inc(s["x_lo_ready"], 1)

                def choose(b, steps):
                    dve.wait_ge(s["logits"], b + 1)
                    steps.link(nc.vector.tensor_reduce(small_t(0), logits, AX.X, ALU.max))
                    nc.vector.tensor_tensor(big(0), logits, per_e(small_t(0)), ALU.subtract).then_inc(s["shifted"], 1)
                    dve.wait_ge(s["exps"], b + 1)
                    steps.link(nc.vector.tensor_reduce(small_t(1), big(1), AX.X, ALU.add))
                    steps.link(nc.vector.reciprocal(small_t(2), small_t(1)))
                    steps.link(nc.vector.tensor_tensor(big(2), big(1), per_e(small_t(2)), ALU.mult))
                    other = big(2).unsqueeze(2).broadcast_to([P, TT, E, E])
                    own = big(2).unsqueeze(3).broadcast_to([P, TT, E, E])
                    steps.mark(nc.vector.tensor_tensor(pair_gt[:], other, own, ALU.is_gt))
                    steps.link(nc.vector.tensor_tensor(pair_ge[:], other, own, ALU.is_ge))
                    steps.link(nc.vector.tensor_tensor(pair_ge[:], pair_ge[:],
                                                       lower[:].unsqueeze(1).broadcast_to([P, TT, E, E]), ALU.mult))
                    steps.link(nc.vector.tensor_tensor(pair_gt[:], pair_gt[:], pair_ge[:], ALU.max))
                    steps.link(nc.vector.tensor_reduce(big(3), pair_gt[:], AX.X, ALU.add))
                    nc.vector.tensor_scalar(mask_b[:], big(3), float(TOPK), None, ALU.is_lt).then_inc(s["masks"], 1)
                    dve.wait_ge(s["masks"], b + 1)

                def weigh(b, steps):
                    steps.link(nc.vector.tensor_tensor(big(4), big(2), mask_b[:], ALU.mult))
                    steps.link(nc.vector.tensor_reduce(small_t(3), big(4), AX.X, ALU.add))
                    steps.link(nc.vector.tensor_scalar(small_t(4), small_t(3), 1e-20, None, ALU.add))
                    steps.link(nc.vector.reciprocal(small_t(5), small_t(4)))
                    steps.link(nc.vector.tensor_tensor(big(5), big(4), per_e(small_t(5)), ALU.mult))
                    dve.wait_ge(s["pos"], b + 1)
                    steps.link(nc.vector.scalar_tensor_tensor(big(6), logits, float(CAPACITY), big(5),
                                                              ALU.is_lt, ALU.mult))
                    steps.link(nc.vector.tensor_copy(comb3[:, :, 0, :], big(6)))
                    steps.link(nc.vector.tensor_tensor(big(7), big(6), comb3[:, :, 0, :], ALU.subtract))
                    steps.link(nc.vector.tensor_copy(comb3[:, :, 1, :], big(7)))
                    nc.vector.tensor_tensor(comb3[:, :, 2, :], big(7), comb3[:, :, 1, :],
                                            ALU.subtract).then_inc(s["comb_parts"], 1)
                    steps.mark(nc.vector.tensor_reduce(tile_n[:], mask_b[:].rearrange("p t e -> p e t"),
                                                       AX.X, ALU.add))

                def count_tokens(steps):
                    steps.wait()
                    steps.link(nc.vector.tensor_tensor(count[:], count[:], tile_n[:], ALU.add))
                    steps.mark(nc.vector.tensor_copy(count_b[:], count[:]))

                def combine_ready(b):
                    dve.wait_ge(s["comb_ps"], b + 1)
                    nc.vector.tensor_copy(comb_t[0:SPLIT3 * E, :], M_comb).then_inc(s["comb_ready"], 1)

                def gated(b, k):
                    dve.wait_ge(s["silu"], b * GROUPS + (k + 1))
                    if k >= NSH + 2:
                        dve.wait_ge(s["hidden"], b * E + (k - NSH - 1))
                    dst = hid if k < NSH else prod
                    nc.vector.tensor_tensor(dst[:, k % 2, :], act_g[:, k % 2, :], U[k % 2][:],
                                            ALU.mult).then_inc(s["gated"], 1)

                def weighted(b, k):
                    dve.wait_ge(s["weight_ps"], b * E + (k - NSH + 1))
                    dve.wait_ge(s["gated"], b * GROUPS + (k + 1))
                    dve.wait_ge(s["hid_lo_ready"], b * GROUPS + (k - 1))
                    nc.vector.tensor_tensor(hid[:, k % 2, :], prod[:, k % 2, :], C[k % 2][:],
                                            ALU.mult).then_inc(s["hidden"], 1)

                if tag == "f1":
                    dve.wait_ge(in_x, 16)
                steps = Steps(dve, step_sem)
                steps.mark(nc.vector.memset(count[:], 0.0))
                steps.mark(nc.vector.memset(count_b[:], 0.0))
                layer_norm(steps, lambda t: x_tok[:, 0, t, :]).then_inc(s["xn_ready"], 1)
                x_low(0)
                choose(0, steps)
                gated(0, 0)
                weigh(0, steps)
                gated(0, 1)
                count_tokens(steps)
                combine_ready(0)
                first, per = steps.n, LN_STEPS + ROUTE_STEPS
                with dve.Fori(0, B) as b:
                    steps = Steps(dve, step_sem, b * per + first)
                    stage = 0
                    for k in range(2, GROUPS):
                        gated(b, k)
                        if k == 2 and tag == "f1":
                            dve.wait_ge(in_x, 16 * B)
                        if stage < LN_STAGES - 1:
                            norm_stage(steps, stage, x_tile((b + 1) & (B - 1)))
                            stage += 1
                        if k - 1 >= NSH:
                            weighted(b, k - 1)
                        while stage < min(LN_STAGES - 1, 2 * (k - 1)):
                            norm_stage(steps, stage, x_tile((b + 1) & (B - 1)))
                            stage += 1
                        if k == GROUPS - 1:
                            while stage < LN_STAGES:
                                ins = norm_stage(steps, stage, x_tile((b + 1) & (B - 1)))
                                stage += 1
                            ins.then_inc(s["xn_ready"], 1)
                    weighted(b, GROUPS - 1)
                    x_low(b + 1)
                    choose(b + 1, steps)
                    gated(b + 1, 0)
                    weigh(b + 1, steps)
                    gated(b + 1, 1)
                    count_tokens(steps)
                    dve.wait_ge(s["yt_ps"], b + 1)
                    xb = x_tok[:, bass.ds(b, 1), :, :].rearrange("p a t d -> p (a t d)")
                    nc.vector.tensor_tensor(xb, YT[:], xb, ALU.add).then_inc(s["x_done"], 1)
                    combine_ready(b + 1)
                    dve.wait_ge(s["x_done"], b + 1)
                    assert steps.n == per, (steps.n, per)

            def pool(pool):
                def hidden_low(b, k):
                    pool.wait_ge(s["hid_hi_ready"], b * GROUPS + (k + 1))
                    if k >= 2:
                        pool.wait_ge(s["y_ps"], b * GROUPS + (k - 1))
                    nc.gpsimd.tensor_tensor(hid_lo[:, k % 2, :], hid[:, k % 2, :], hid_hi[:, k % 2, :],
                                            ALU.subtract).then_inc(s["hid_lo_ready"], 1)

                hidden_low(0, 0)
                with pool.Fori(0, B) as b:
                    for k in range(1, GROUPS):
                        hidden_low(b, k)
                    hidden_low(b + 1, 0)

            def sync(sp):
                if last:
                    with sp.Fori(0, B) as b:
                        sp.wait_ge(s["x_done"], b + 1)
                        sp.dma_start(out[bass.ds(b, 1)].rearrange("a (t p) d -> p (a t) d", p=P),
                                     x_tok[:, bass.ds(b, 1)].rearrange("p a t d -> p (a t) d")).then_inc(stored, 16)
                    sp.wait_ge(stored, 16 * B)
            return dict(tensor=pe, scalar=act, vector=dve, gpsimd=pool, sync=sync)

        def attention():
            s = {n: sem(f"att_{n}") for n in (
                "xn_ready", "xt_ps", "x_hi_ready", "x_lo_ready", "qk_ps", "roped", "added", "own_high",
                "v_ps", "v_ready", "scores", "maxes", "probs", "pt_ps", "pt_ready", "o_ps",
                "rec_ready", "rec_t_ps", "rec_t_ready", "rec_ps", "rec_copied", "o_ready",
                "y_ps", "y_copied", "yt_ps", "x_done")}
            S, PT = (bank[0], bank[1]), (bank[2], bank[3])
            O, R, J, Y = bank[4], bank[5], bank[6], bank[7]
            R_t = R[0:SPLIT3 * UNITS, 0:P // 2].bitcast(BF16)
            rec_t = comb_t[:, 0:P]
            step_sem, pool_step = dve_step["att"], sem("pool_step")
            ORDER = (2, 3, 0, 1)
            OWN = (slice(0, DH), slice(DH, P))
            FAR = (slice(DH, P), slice(0, DH))
            PARTS_AT = {0: (0,), 1: (1,), 2: (2, 3)}
            PART_BANK = (J, R, J, R)
            PV_AT = {3: 0, 4: 1, 5: 2, 7: 3}
            V_AT = (3, 4, 5, 6)
            V_PAIR = {PAIRS - 1: 0, 2: 1}
            OPEN = 3
            FRONT_PAIR, FRONT_UNIT = PAIRS - 2, 3
            NORM_AT = [(j, u) for j in range(OPEN, FRONT_PAIR) for u in (1, 3, 5, 6, 7)] + [(FRONT_PAIR, 1)]
            REC_STEPS = 5
            nothing = lambda b, j: None

            def pairs(eng, pair, end):
                for j in range(OPEN):
                    pair(0, j, min(j, 2), True)
                with eng.Fori(0, B - 1) as b:
                    for j in range(OPEN, PAIRS):
                        pair(b, j, 2, True)
                    for j in range(OPEN):
                        pair(b + 1, j, 2, True)
                for j in range(OPEN, PAIRS):
                    pair(B - 1, j, 2, False)
                end(B - 1)

            def unit_of(b, j, u):
                return b * (PAIRS * UNITS) + (j * UNITS + u)

            def pe(pe):
                def front(b):
                    pe.wait_ge(s["xn_ready"], b + 1)
                    for t in range(TT):
                        ins = nc.tensor.transpose(J[:, t * P:(t + 1) * P], xn[:, t, :], ident[:])
                    ins.then_inc(s["xt_ps"], 1)

                def roped(b, j, i):
                    pe.wait_ge(s["roped"], b * (PAIRS * PARTS) + (j * PARTS + i + 1))

                def project(b, j, i):
                    if i >= 2:
                        roped(b, j, i - 2)
                    for n, (w, a) in enumerate(((qk_hi, x_hi), (qk_lo, x_hi), (qk_hi, x_lo))):
                        ins = nc.tensor.matmul(PART_BANK[i][:], w[:, j % PAIRS, ORDER[i], :], a[:],
                                               start=(n == 0), stop=(n == 2))
                    ins.then_inc(s["qk_ps"], 1)

                def values(b, half, t):
                    if t:
                        pe.wait_ge(s["v_ready"], b * (2 * TT) + (half * TT + t))
                    cols = slice(half * T, (half + 1) * T)
                    tok = slice(t * P, (t + 1) * P)
                    for n, (a, w) in enumerate(((x_hi, v_hi), (x_lo, v_hi), (x_hi, v_lo))):
                        ins = nc.tensor.matmul(J[:], a[:, tok], w[:, cols], start=(n == 0), stop=(n == 2))
                    ins.then_inc(s["v_ps"], 1)

                def scores(b, j, u, first):
                    h, qt = divmod(u, TT)
                    if u == 0:
                        pe.wait_ge(q_split, b * PAIRS + (j + 1))
                        pe.wait_ge(k_own_low, b * PAIRS + (j + 1))
                        pe.wait_ge(k_far_high, b * PAIRS + (j + 1))
                    if not first or u >= 2:
                        pe.wait_ge(s["probs"], unit_of(b, j, u - 1))
                    for i, k in enumerate((k_hh, k_ll)):
                        ins = nc.tensor.matmul(S[u % 2][:], q_st[:, j % 2, h, qt * P:(qt + 1) * P],
                                               k[:, j % 2, h, :], start=(i == 0), stop=(i == 1))
                    ins.then_inc(s["scores"], 1)

                def transposes(b, j, u, first=False):
                    pe.wait_ge(s["probs"], unit_of(b, j, u + 1))
                    if not first or u >= 2:
                        pe.wait_ge(s["pt_ready"], unit_of(b, j, u - 1))
                    for k in range(TT):
                        ins = nc.tensor.transpose(PT[u % 2][:, k * P:(k + 1) * P],
                                                  prob[:, u % NP, k * P:(k + 1) * P], ident[:])
                    ins.then_inc(s["pt_ps"], 1)

                def apply_v(b, j, k, first=False):
                    if k == 0:
                        pe.wait_ge(s["pt_ready"], unit_of(b, j + 1, 0))
                        if not first:
                            pe.wait_ge(s["o_ready"], b * PAIRS + j)
                    for h in range(2):
                        n = 2 * (j % PAIRS) + h
                        ins = nc.tensor.matmul(O[h * DH:(h + 1) * DH, :], v_all[:, k, n * DH:(n + 1) * DH],
                                               pt[:, j % 2, h, k, :], start=(k == 0), stop=(k == TT - 1))
                    if k == TT - 1:
                        ins.then_inc(s["o_ps"], 1)

                def transpose_reciprocals(b, j):
                    pe.wait_ge(s["rec_ready"], b * PAIRS + (j + 1))
                    nc.tensor.transpose(R_t, rec3[:, j % 2].rearrange("p a h t -> p (a h t)"), ident_b[:])\
                      .then_inc(s["rec_t_ps"], 1)

                def reciprocals(b, j):
                    pe.wait_ge(s["rec_t_ready"], b * PAIRS + (j + 1))
                    for qt in range(TT):
                        for h in range(2):
                            ins = nc.tensor.matmul(R[h * DH:(h + 1) * DH, qt * P:(qt + 1) * P],
                                                   sel_b[:, h * TT + qt, 0:DH], rec_t, start=True, stop=True)
                    ins.then_inc(s["rec_ps"], 1)

                def project_out(b, j):
                    pe.wait_ge(s["o_ready"], b * PAIRS + (j + 1))
                    j = j % PAIRS
                    nc.tensor.matmul(Y[:], wo[:, j, :], o_t[:, j % 2, :], start=(j == 0),
                                     stop=(j == PAIRS - 1)).then_inc(s["y_ps"], 1)

                def transpose_y(b):
                    pe.wait_ge(s["y_copied"], b)
                    for t in range(TT):
                        ins = nc.tensor.transpose(Y[:, t * P:(t + 1) * P], y_t[:, t * P:(t + 1) * P], ident[:])
                    ins.then_inc(s["yt_ps"], 1)

                def pair(b, j, before, more):
                    nxt = more or j < PAIRS - 1
                    batch_before = not (isinstance(b, int) and b == 0)
                    for u in range(UNITS):
                        scores(b, j, u, before == 0)
                        if nxt:
                            if u == 0 and j == PAIRS - 1:
                                pe.wait_ge(s["x_lo_ready"], b + 2)
                            if u == 0 and j in (0, 3):
                                pe.wait_ge(s["v_ready"], b * (2 * TT) + (TT if j == 0 else 2 * TT))
                            if u == 1 and before == 2:
                                pe.wait_ge(s["rec_copied"], b * PAIRS + (j - 1))
                            for i in PARTS_AT.get(u, ()):
                                project(b, j + 1, i)
                        if (j, u) == (FRONT_PAIR, FRONT_UNIT) and more:
                            roped(b, j + 1, 2)
                            front(b + 1)
                        if j in V_PAIR and u in V_AT and (more or j != PAIRS - 1):
                            if u == V_AT[0]:
                                roped(b, j + 1, 2)
                            values(b + 1 if j == PAIRS - 1 else b, V_PAIR[j], V_AT.index(u))
                        if u >= LAG:
                            transposes(b, j, u - LAG, before == 0)
                        elif before:
                            transposes(b, j - 1, UNITS - LAG + u)
                        if before and u in PV_AT:
                            apply_v(b, j - 1, PV_AT[u], before == 1)
                        if before and u == 5:
                            if nxt:
                                roped(b, j + 1, 3)
                            transpose_reciprocals(b, j - 1)
                        if before and u == 6:
                            reciprocals(b, j - 1)
                        if before == 2 and u == 6:
                            if j == 2 and batch_before:
                                pe.wait_ge(s["x_done"], b)
                            project_out(b, j - 2)
                        if j == 2 and u == 1 and batch_before:
                            transpose_y(b)

                def end(b):
                    j = PAIRS - 1
                    for u in range(UNITS - LAG, UNITS):
                        transposes(b, j, u)
                    pe.wait_ge(s["rec_copied"], b * PAIRS + j)
                    transpose_reciprocals(b, j)
                    project_out(b, j - 1)
                    for k in range(TT):
                        apply_v(b, j, k)
                    reciprocals(b, j)
                    project_out(b, j)
                    transpose_y(b + 1)

                pe.wait_ge(w_lo_ready, 5)
                front(0)
                pe.wait_ge(s["x_lo_ready"], 1)
                for i in range(PARTS):
                    project(0, 0, i)
                roped(0, 0, 2)
                for t in range(TT):
                    values(0, 0, t)
                pairs(pe, pair, end)

            def act(act):
                def x_high(b):
                    act.wait_ge(s["xt_ps"], b + 1)
                    nc.scalar.activation(x_hi[:], J[:], ACT.Copy).then_inc(s["x_hi_ready"], 1)

                def values(b, half, t):
                    act.wait_ge(s["v_ps"], b * (2 * TT) + (half * TT + t + 1))
                    nc.scalar.activation(v_all[:, t, half * T:(half + 1) * T], J[:], ACT.Copy)\
                      .then_inc(s["v_ready"], 1)

                def exponentials(b, j, u, first):
                    act.wait_ge(s["maxes"], unit_of(b, j, u + 1))
                    if not first or u >= NP:
                        act.wait_ge(s["pt_ps"], unit_of(b, j, u + 1 - NP))
                    nc.scalar.activation(prob[:, u % NP, :], S[u % 2][:], ACT.Exp,
                                         bias=neg_max[:, j % 2, u:u + 1],
                                         accum_out=den[:, j % 2, u:u + 1]).then_inc(s["probs"], 1)

                def move(b, j, u):
                    h, qt = divmod(u, TT)
                    act.wait_ge(s["pt_ps"], unit_of(b, j, u + 1))
                    nc.scalar.activation(pt[:, j % 2, h, :, qt * P:(qt + 1) * P],
                                         PT[u % 2][:].rearrange("p (k q) -> p k q", q=P),
                                         ACT.Copy).then_inc(s["pt_ready"], 1)

                def far_high(b, j):
                    act.wait_ge(s["added"], b * (2 * PAIRS) + (2 * j + 1))
                    for h in range(2):
                        ins = nc.scalar.activation(k_hh[FAR[h], j % 2, h, :], rope_tmp[OWN[h], 2, :], ACT.Copy)
                    ins.then_inc(k_far_high, 1)

                def copy_reciprocals(b, j):
                    act.wait_ge(s["rec_t_ps"], b * PAIRS + (j + 1))
                    nc.scalar.activation(rec_t[0:SPLIT3 * UNITS, :], R_t, ACT.Copy).then_inc(s["rec_t_ready"], 1)

                def spread_reciprocals(b, j, before):
                    act.wait_ge(s["rec_ps"], b * PAIRS + (j + 1))
                    if before == 2:
                        act.wait_ge(s["o_ready"], b * PAIRS + j)
                    nc.scalar.activation(rec_all[:], R[:], ACT.Copy).then_inc(s["rec_copied"], 1)

                def copy_y(b):
                    act.wait_ge(s["y_ps"], b * PAIRS)
                    nc.scalar.activation(y_t, Y[:], ACT.Identity, bias=bo[:, 0:1]).then_inc(s["y_copied"], 1)

                def pair(b, j, before, more):
                    nxt = more or j < PAIRS - 1
                    batch_before = not (isinstance(b, int) and b == 0)
                    for u in range(UNITS):
                        exponentials(b, j, u, before == 0)
                        if j in V_PAIR and u in V_AT and (more or j != PAIRS - 1):
                            values(b + 1 if j == PAIRS - 1 else b, V_PAIR[j], V_AT.index(u))
                        if (j, u) == (FRONT_PAIR, FRONT_UNIT) and more:
                            x_high(b + 1)
                        if u >= LAG:
                            move(b, j, u - LAG)
                        elif before:
                            move(b, j - 1, UNITS - LAG + u)
                        if before and u == 5:
                            copy_reciprocals(b, j - 1)
                        if before and u == 7:
                            spread_reciprocals(b, j - 1, before)
                        if nxt and u == 3:
                            far_high(b, j + 1)
                        if j == 1 and u == 7 and batch_before:
                            copy_y(b)

                def end(b):
                    j = PAIRS - 1
                    for u in range(UNITS - LAG, UNITS):
                        move(b, j, u)
                    copy_reciprocals(b, j)
                    spread_reciprocals(b, j, 2)
                    copy_y(b + 1)

                x_high(0)
                act.wait_ge(w_lo_ready, 5)
                far_high(0, 0)
                for t in range(TT):
                    values(0, 0, t)
                pairs(act, pair, end)

            def dve(dve):
                def x_low(b):
                    dve.wait_ge(s["x_hi_ready"], b + 1)
                    nc.vector.tensor_tensor(x_lo[:], J[:], x_hi[:], ALU.subtract).then_inc(s["x_lo_ready"], 1)

                def rope_part(b, j, i):
                    dve.wait_ge(s["qk_ps"], b * (PAIRS * PARTS) + (j * PARTS + i + 1))
                    nc.vector.tensor_tensor(rope_tmp[:, ORDER[i], :], PART_BANK[i][:], rope_t[:, ORDER[i] % 2, :],
                                            ALU.mult).then_inc(s["roped"], 1)

                def k_own_high(b, j):
                    dve.wait_ge(s["added"], b * (2 * PAIRS) + (2 * j + 1))
                    for h in range(2):
                        ins = nc.vector.tensor_copy(k_hh[OWN[h], j % 2, h, :], rope_tmp[OWN[h], 2, :])
                    ins.then_inc(s["own_high"], 1)

                def k_far_low(b, j):
                    dve.wait_ge(s["own_high"], b * PAIRS + (j + 1))
                    for h in range(2):
                        steps.mark(nc.vector.tensor_tensor(k_ll[FAR[h], j % 2, h, :], rope_tmp[OWN[h], 2, :],
                                                           k_hh[OWN[h], j % 2, h, :], ALU.subtract))

                def q_high(b, j):
                    dve.wait_ge(s["added"], b * (2 * PAIRS) + (2 * j + 2))
                    for h in range(2):
                        steps.mark(nc.vector.tensor_copy(q_st[OWN[h], j % 2, h, :], rope_tmp[OWN[h], 0, :]))

                def q_low(b, j):
                    steps.wait()
                    for h in range(2):
                        ins = nc.vector.tensor_tensor(q_st[FAR[h], j % 2, h, :], rope_tmp[OWN[h], 0, :],
                                                      q_st[OWN[h], j % 2, h, :], ALU.subtract)
                    ins.then_inc(q_split, 1)

                def maxima(b, j, u):
                    dve.wait_ge(s["scores"], unit_of(b, j, u + 1))
                    nc.vector.tensor_reduce(neg_max[:, j % 2, u:u + 1], S[u % 2][:], AX.X, ALU.max,
                                            negate=True).then_inc(s["maxes"], 1)

                def reciprocals(b, j, n):
                    parts = [rec3[:, j % 2, a].rearrange("p h t -> p (h t)") for a in range(SPLIT3)]
                    steps.wait()
                    if n == 0:
                        dve.wait_ge(s["probs"], unit_of(b, j + 1, 0))
                        steps.mark(nc.vector.reciprocal(rec[:, 0, :], den[:, j % 2, :]))
                    elif n == 1:
                        steps.mark(nc.vector.tensor_copy(parts[0], rec[:, 0, :]))
                    elif n == 2:
                        steps.mark(nc.vector.tensor_tensor(rec[:, 1, :], rec[:, 0, :], parts[0], ALU.subtract))
                    elif n == 3:
                        steps.mark(nc.vector.tensor_copy(parts[1], rec[:, 1, :]))
                    else:
                        nc.vector.tensor_tensor(parts[2], rec[:, 1, :], parts[1],
                                                ALU.subtract).then_inc(s["rec_ready"], 1)

                def normalise(b, j):
                    dve.wait_ge(s["o_ps"], b * PAIRS + (j + 1))
                    dve.wait_ge(s["rec_copied"], b * PAIRS + (j + 1))
                    nc.vector.tensor_tensor(o_t[:, j % 2, :], O[:], rec_all[:], ALU.mult).then_inc(s["o_ready"], 1)

                def residual(b):
                    dve.wait_ge(s["yt_ps"], b)
                    which = slice(b - 1, b) if isinstance(b, int) else bass.ds(b - 1, 1)
                    xb = x_tok[:, which, :, :].rearrange("p a t d -> p (a t d)")
                    nc.vector.tensor_tensor(xb, Y[:], xb, ALU.add).then_inc(s["x_done"], 1)
                    dve.wait_ge(s["x_done"], b)

                def pair(b, j, before, more):
                    nxt = more or j < PAIRS - 1
                    batch_before = not (isinstance(b, int) and b == 0)
                    for u in range(UNITS):
                        maxima(b, j, u)
                        if before and 1 <= u < REC_STEPS:
                            reciprocals(b, j - 1, u)
                        if nxt:
                            for i in PARTS_AT.get(u, ()):
                                rope_part(b, j + 1, i)
                            {3: k_own_high, 4: k_far_low, 5: q_high, 6: q_low}.get(u, nothing)(b, j + 1)
                        if before == 2 and u == 0:
                            normalise(b, j - 2)
                        if before and u == 0:
                            reciprocals(b, j - 1, 0)
                        if (j, u) == (FRONT_PAIR, FRONT_UNIT) and more:
                            x_low(b + 1)
                        if j == 2 and u == 2 and batch_before:
                            residual(b)
                        if more and (j, u) in NORM_AT:
                            ins = norm_stage(steps, NORM_AT.index((j, u)), x_tile(b + 1))
                            if ins is not None:
                                ins.then_inc(s["xn_ready"], 1)

                def end(b):
                    j = PAIRS - 1
                    normalise(b, j - 1)
                    for n in range(REC_STEPS):
                        reciprocals(b, j, n)
                    normalise(b, j)
                    residual(b + 1)

                assert len(NORM_AT) == LN_STAGES
                steps = Steps(dve, step_sem)
                layer_norm(steps, lambda t: x_tok[:, 0, t, :]).then_inc(s["xn_ready"], 1)
                x_low(0)
                dve.wait_ge(w_lo_ready, 5)
                for i in range(PARTS):
                    rope_part(0, 0, i)
                k_own_high(0, 0)
                k_far_low(0, 0)
                q_high(0, 0)
                q_low(0, 0)
                for j in range(OPEN):
                    pair(0, j, min(j, 2), True)
                first = steps.n
                per = LN_STEPS + (REC_STEPS - 1 + 4) * PAIRS
                with dve.Fori(0, B - 1) as b:
                    steps = Steps(dve, step_sem, b * per + first)
                    for j in range(OPEN, PAIRS):
                        pair(b, j, 2, True)
                    for j in range(OPEN):
                        pair(b + 1, j, 2, True)
                    assert steps.n == per, (steps.n, per)
                steps = Steps(dve, step_sem, (B - 1) * per + first)
                for j in range(OPEN, PAIRS):
                    pair(B - 1, j, 2, False)
                end(B - 1)

            def pool(pool):
                def rotate(g, parity):
                    tmp = lambda part: rope_tmp[:, part, :]
                    steps = Steps(pool, pool_step, g * 3)
                    pool.wait_ge(s["roped"], g * PARTS + 2)
                    steps.link(nc.gpsimd.tensor_tensor(tmp(3), tmp(3), fenc[:, 1, :], ALU.add))
                    nc.gpsimd.tensor_tensor(tmp(2), tmp(2), tmp(3), ALU.add).then_inc(s["added"], 1)
                    pool.wait_ge(s["roped"], g * PARTS + PARTS)
                    steps.link(nc.gpsimd.tensor_tensor(tmp(1), tmp(1), fenc[:, 0, :], ALU.add))
                    nc.gpsimd.tensor_tensor(tmp(0), tmp(0), tmp(1), ALU.add).then_inc(s["added"], 1)
                    pool.wait_ge(s["added"], g * 2 + 2)
                    pool.wait_ge(s["own_high"], g + 1)
                    steps.link(nc.gpsimd.tensor_tensor(k_ll[OWN[0], parity, 0, :], tmp(2)[OWN[0]],
                                                       k_hh[OWN[0], parity, 0, :], ALU.subtract))
                    nc.gpsimd.tensor_tensor(k_ll[OWN[1], parity, 1, :], tmp(2)[OWN[1]],
                                            k_hh[OWN[1], parity, 1, :], ALU.subtract).then_inc(k_own_low, 1)
                    pool.wait_ge(k_own_low, g + 1)

                pool.wait_ge(fenc_ready, 2)
                with pool.Fori(0, B * PAIRS // 2) as two:
                    rotate(two * 2, 0)
                    rotate(two * 2 + 1, 1)
            return dict(tensor=pe, scalar=act, vector=dve, gpsimd=pool)

        def x_tile(b):
            return lambda t: x_tok[:, bass.ds(b, 1), t, :].rearrange("p a d -> p (a d)")

        ffn1, att, ffn2 = ffn("f1", False), attention(), ffn("f2", True)

        @block.sync
        def _(sp):
            setup_sync(sp)
            ffn2["sync"](sp)

        @block.scalar
        def _(act):
            setup_act(act)
            ffn1["scalar"](act)
            att["scalar"](act)
            ffn2["scalar"](act)

        @block.vector
        def _(dve):
            setup_dve(dve)
            ffn1["vector"](dve)
            att["vector"](dve)
            ffn2["vector"](dve)

        @block.tensor
        def _(pe):
            setup_pe(pe)
            ffn1["tensor"](pe)
            att["tensor"](pe)
            ffn2["tensor"](pe)

        @block.gpsimd
        def _(pool):
            ffn1["gpsimd"](pool)
            att["gpsimd"](pool)
            ffn2["gpsimd"](pool)


def kernel(L0_attn_x, L0_attn_w_qkv, L0_attn_w_fproj, L0_attn_b_fproj, L0_attn_w_out, L0_attn_b_out,
           L0_ffn_gate_w, L0_ffn_we_gate, L0_ffn_we_up, L0_ffn_we_down, L0_ffn_ws_gate, L0_ffn_ws_up,
           L0_ffn_ws_down):
    import ml_dtypes
    import numpy as np
    import concourse.bacc as bacc
    from concourse.bass_utils import run_bass_kernel_spmd

    a = np.asarray
    wqkv = a(L0_attn_w_qkv).reshape(3, HEADS, DH, D)
    half = DH // 2
    turned = np.r_[2 * np.arange(half) + 1, 2 * np.arange(half)]
    qk = np.stack([wqkv[0], wqkv[0][:, turned], wqkv[1], wqkv[1][:, turned]])
    qk = qk.reshape(PARTS, PAIRS, P, D).transpose(3, 1, 0, 2)
    gate = np.concatenate([a(L0_ffn_ws_gate).reshape(NSH, P, D), a(L0_ffn_we_gate)])
    up = np.concatenate([a(L0_ffn_ws_up).reshape(NSH, P, D), a(L0_ffn_we_up)])
    ws_down = a(L0_ffn_ws_down).reshape(D, NSH, P).transpose(2, 1, 0)
    we_down = a(L0_ffn_we_down).transpose(2, 0, 1)
    fproj = a(L0_attn_w_fproj).T

    freqs = np.float32(10000.0) ** (-np.arange(0, DH, 2, dtype=np.float32) / np.float32(DH))
    pos = np.arange(T, dtype=np.float32)
    angles = (pos[:, None] * freqs[None, :]).astype(np.float32).astype(np.float64)
    cos = np.repeat(np.cos(angles), 2, axis=1).T
    sin = np.repeat(np.sin(angles), 2, axis=1).T * np.where(np.arange(DH) < half, -1.0, 1.0)[:, None]
    rope = np.stack([cos, sin]).astype(np.float32)
    rope = np.concatenate([rope, rope], axis=1).transpose(1, 0, 2)
    nf = np.arange(1, NF // 2 + 1, dtype=np.float32)
    fa = (nf[:, None] * pos[None, :]).astype(np.float64)
    fourier = np.concatenate([np.sin(fa), np.cos(fa)]).astype(np.float32)
    ident = np.eye(P, dtype=np.float32)
    lower = np.zeros((P, P), np.float32)
    lower[:, :E * E] = (np.arange(E)[None, :] < np.arange(E)[:, None]).reshape(-1)
    before = np.triu(np.ones((P, P), np.float32), 1)
    sel = np.zeros((P, E, P), np.float32)
    for r in range(SPLIT3 * E):
        sel[r, r % E] = 1.0

    bf = ml_dtypes.bfloat16
    arrays = {
        "x": a(L0_attn_x),
        "w_gate_up": np.concatenate([gate, up]).transpose(2, 0, 1).reshape(P, -1),
        "w_down": np.concatenate([ws_down, we_down], axis=1).reshape(P, -1),
        "gate_t": a(L0_ffn_gate_w).T,
        "w_qk": qk.reshape(P, -1),
        "w_v": wqkv[2].reshape(INNER, D).T,
        "w_out": a(L0_attn_w_out).reshape(D, PAIRS, P).transpose(2, 1, 0).reshape(P, -1),
        "b_out": a(L0_attn_b_out)[:, None],
        "fproj": np.concatenate([fproj, fproj], axis=1),
        "bproj": np.concatenate([a(L0_attn_b_fproj)] * 2)[:, None],
        "rope": rope.reshape(P, -1),
        "fourier": fourier,
        "consts": np.stack([ident, lower]),
        "consts_b": np.stack([before, ident]).astype(bf),
        "sel": sel.reshape(P, -1).astype(bf),
    }
    nc = bacc.Bacc("TRN2", target_bir_lowering=False, num_devices=1)
    inputs, args = {}, []
    for name, v in arrays.items():
        v = np.ascontiguousarray(v)
        inputs[f"in_{name}"] = v
        args.append(nc.dram_tensor(f"in_{name}", v.shape, mybir.dt.from_np(v.dtype), kind="ExternalInput").ap())
    out = nc.dram_tensor("out", (B, T, D), F32, kind="ExternalOutput").ap()
    macaron(nc, *args, out)
    r = run_bass_kernel_spmd(nc, [inputs], core_ids=[0])
    return r.results[0]["out"]
```

```python
from contextlib import ExitStack

import concourse.bass as bass
from concourse import mybir

F32 = mybir.dt.float32
F32R = mybir.dt.float32r
BF16 = mybir.dt.bfloat16
I32 = mybir.dt.int32
ALU = mybir.AluOpType
ACT = mybir.ActivationFunctionType
AX = mybir.AxisListType

P = 128
B, T, D = 8, 512, 128
TT = T // P
HEADS, DH = 16, 64
INNER = HEADS * DH
PAIRS = HEADS // 2
NF = 32
E, NSH, TOPK = 8, 2, 2
GROUPS = NSH + E
CAPACITY = -(-5 * B * T * TOPK // (4 * E))
EPS = 1e-5
QSCALE = DH ** -0.5
UNITS = 2 * TT
PARTS = 4
LAG = 3
NH = 5
NP = 4
SPLIT3 = 3
RSQRT_MAGIC = 0x5F3759DF
NEWTON = 3
EARLY_GROUPS = 2
ROUTE_STEPS = 21
LN_STAGES = 7 + 3 * NEWTON
LN_STEPS = TT + 7 + 2 + 4 * NEWTON + TT - 1


class Steps:

    def __init__(self, eng, sem, base=0):
        self.eng, self.sem, self.base, self.n = eng, sem, base, 0

    def mark(self, ins):
        ins.then_inc(self.sem, 1)
        self.n += 1

    def wait(self):
        self.eng.wait_ge(self.sem, self.base + self.n)

    def link(self, ins):
        self.mark(ins)
        self.wait()


def macaron(nc, x, w_gate_up, w_down, gate_t, w_qk, w_v, w_out, b_out, fproj, bproj,
            rope, fourier, consts, consts_b, sel, out):
    with ExitStack() as ctx:
        def sb(name, shape, dt=F32):
            return ctx.enter_context(nc.sbuf_tensor(name, shape, dt))

        def sem(name):
            return ctx.enter_context(nc.semaphore(name))

        x_tok = sb("x_tok", [P, B, TT, D])
        gu_hi = sb("gu_hi", [P, 2 * GROUPS, P], F32R)
        gu_lo = sb("gu_lo", [P, 2 * GROUPS, P], F32R)
        down_hi = sb("down_hi", [P, GROUPS, D], F32R)
        down_lo = sb("down_lo", [P, GROUPS, D], F32R)
        gate_w = sb("gate_w", [P, E])
        gate_hi = sb("gate_hi", [P, E], F32R)
        gate_lo = sb("gate_lo", [P, E], F32R)
        qk_hi = sb("qk_hi", [P, PAIRS, PARTS, P], F32R)
        qk_lo = sb("qk_lo", [P, PAIRS, PARTS, P], F32R)
        v_hi = sb("v_hi", [P, INNER], F32R)
        v_lo = sb("v_lo", [P, INNER], F32R)
        wo = sb("wo", [P, PAIRS, D])
        bo = sb("bo", [P, 1])
        rope_t = sb("rope_t", [P, 2, T])
        fenc = sb("fenc", [P, 2, T])
        ident = sb("ident", [P, P])
        ident_b = sb("ident_b", [P, P], BF16)
        before_b = sb("before_b", [P, P], BF16)
        ones_b = sb("ones_b", [P, P], BF16)
        lower = sb("lower", [P, E, E])
        sel_b = sb("sel_b", [P, E, P], BF16)
        x_hi = sb("x_hi", [P, T], F32R)
        x_lo = sb("x_lo", [P, T], F32R)
        xn = sb("xn", [P, TT, D])
        y_t = xn[:].rearrange("p t d -> p (t d)")
        stats = sb("stats", [P, TT, 6])
        mv = sb("mv", [P, TT, 2])
        mean = sb("mean", [P, TT])
        ve = sb("ve", [P, TT])
        rs = sb("rs", [P, TT])
        rsi = sb("rsi", [P, TT], I32)
        nt = sb("nt", [P, 3, TT])
        work = sb("work", [P, 3 * 4096])
        v_all = work[:, 0:4096].rearrange("p (t n) -> p t n", t=TT)
        pt = work[:, 4096:].rearrange("p (g h k q) -> p g h k q", g=2, h=2, k=TT)
        st_qk = work[:, 0:PAIRS * PARTS * P].rearrange("p (a b n) -> p a b n", a=PAIRS, b=PARTS)
        st_v = work[:, 4096:4096 + INNER]
        st_gu = work[:, 4096 + INNER:4096 + INNER + 2 * GROUPS * P]
        prob = sb("prob", [P, NP, T])
        act_g, prod = prob[:, 0:2, :], prob[:, 2:4, :]
        comb_t = sb("comb_t", [P, T], BF16)
        route = sb("route", [P, 8, TT, E])
        pair_gt = sb("pair_gt", [P, TT, E, E])
        pair_ge = sb("pair_ge", [P, TT, E, E])
        small = sb("small", [P, 8, TT])
        mask_b = sb("mask_b", [P, TT, E], BF16)
        count_b = sb("count_b", [P, E], BF16)
        count = sb("count", [P, E])
        tile_n = sb("tile_n", [P, E])
        comb3 = sb("comb3", [P, TT, SPLIT3, E], BF16)
        o_t = sb("o_t", [P, 2, T])
        q_st = sb("q_st", [P, 2, 2, T], F32R)
        k_hh = sb("k_hh", [P, 2, 2, T], F32R)
        k_ll = sb("k_ll", [P, 2, 2, T], F32R)
        hid_hi, hid_lo = k_hh[:, 0], k_ll[:, 0]
        rope_tmp = sb("rope_tmp", [P, PARTS, T])
        neg_max = sb("neg_max", [P, 2, UNITS])
        den = sb("den", [P, 2, UNITS])
        rec = sb("rec", [P, 3, UNITS])
        rec3 = sb("rec3", [P, 2, SPLIT3, 2, TT], BF16)
        rec_all = sb("rec_all", [P, T])
        st_down = work[:, 4096 + INNER + 2 * GROUPS * P:4096 + INNER + 3 * GROUPS * P]
        free = 4096 + INNER + 3 * GROUPS * P
        fourier_s, fproj_s = work[0:NF, free:free + T], work[0:NF, free + T:free + T + P]
        bproj_s = sb("bproj_s", [P, 1])

        bank = [ctx.enter_context(nc.psum_tensor(f"bank{i}", [P, T], F32)) for i in range(8)]

        in_x, in_ffn, in_att, in_small = sem("in_x"), sem("in_ffn"), sem("in_att"), sem("in_small")
        in_first, in_fourier, in_x0 = sem("in_first"), sem("in_fourier"), sem("in_x0")
        consts_ready = sem("consts_ready")
        w_hi_ready, w_lo_ready = sem("w_hi_ready"), sem("w_lo_ready")
        fenc_ps, fenc_ready = sem("fenc_ps"), sem("fenc_ready")
        dve_step = {ph: sem(f"dve_step_{ph}") for ph in ("setup", "f1", "att", "f2")}
        stored = sem("stored")
        q_split = sem("q_split")
        k_own_low = sem("k_own_low")
        k_far_high = sem("k_far_high")
        x_moved = sem("x_moved")

        block = ctx.enter_context(nc.Block())

        def setup_sync(sp):
            sp.dma_start(x_tok[:, 0], x[0].rearrange("(t p) d -> p t d", p=P)).then_inc(in_x0, 16)
            sp.dma_start(ident[:], consts[0]).then_inc(in_first, 16)
            sp.dma_start(gate_w[:], gate_t).then_inc(in_first, 16)
            sp.dma_start(st_gu, w_gate_up).then_inc(in_ffn, 16)
            sp.dma_start(fourier_s, fourier).then_inc(in_fourier, 16)
            sp.dma_start(fproj_s, fproj).then_inc(in_fourier, 16)
            sp.dma_start(bproj_s[:], bproj).then_inc(in_fourier, 16)
            sp.dma_start(lower[:].rearrange("p a b -> p (a b)"), consts[1][:, 0:E * E]).then_inc(in_small, 16)
            sp.dma_start(st_down, w_down).then_inc(in_ffn, 16)
            sp.dma_start(before_b[:], consts_b[0]).then_inc(in_small, 16)
            sp.dma_start(ident_b[:], consts_b[1]).then_inc(in_small, 16)
            sp.dma_start(sel_b[:].rearrange("p e m -> p (e m)"), sel).then_inc(in_small, 16)
            for b in range(1, B):
                sp.dma_start(x_tok[:, b], x[b].rearrange("(t p) d -> p t d", p=P)).then_inc(in_x, 16)
            sp.dma_start(work[:, 0:PAIRS * PARTS * P], w_qk).then_inc(in_att, 16)
            sp.dma_start(st_v, w_v).then_inc(in_att, 16)
            sp.dma_start(wo[:].rearrange("p g d -> p (g d)"), w_out).then_inc(in_att, 16)
            sp.dma_start(rope_t[:].rearrange("p a t -> p (a t)"), rope).then_inc(in_att, 16)
            sp.dma_start(bo[:], b_out).then_inc(in_att, 16)

        def setup_act(act):
            act.wait_ge(in_first, 32)
            nc.scalar.activation(gate_hi[:], gate_w[:], ACT.Copy).then_inc(w_hi_ready, 1)
            act.wait_ge(in_fourier, 48)
            act.wait_ge(fenc_ps, 1)
            nc.scalar.activation(fenc[:, 1, :], bank[6][:], ACT.Identity, bias=bproj_s[:, 0:1]).then_inc(fenc_ready, 1)
            act.wait_ge(fenc_ready, 1)
            nc.scalar.activation(fenc[:, 0, :], fenc[:, 1, :], ACT.Copy, scale=QSCALE).then_inc(fenc_ready, 1)

        def ffn_weights_high(act):
            act.wait_ge(in_ffn, 32)
            nc.scalar.activation(gu_hi[:].rearrange("p g n -> p (g n)"), st_gu, ACT.Copy).then_inc(w_hi_ready, 1)
            nc.scalar.activation(down_hi[:].rearrange("p g n -> p (g n)"), st_down, ACT.Copy).then_inc(w_hi_ready, 1)

        def setup_dve(dve):
            nc.vector.memset(ones_b[:], 1.0).then_inc(consts_ready, 1)
            nc.vector.memset(comb_t[:], 0.0).then_inc(consts_ready, 1)

        def gate_low(dve):
            dve.wait_ge(w_hi_ready, 1)
            nc.vector.tensor_tensor(gate_lo[:], gate_w[:], gate_hi[:], ALU.subtract).then_inc(w_lo_ready, 1)

        def gate_up_low(dve):
            dve.wait_ge(w_hi_ready, 2)
            nc.vector.tensor_tensor(gu_lo[:].rearrange("p g n -> p (g n)"), st_gu,
                                    gu_hi[:].rearrange("p g n -> p (g n)"), ALU.subtract).then_inc(w_lo_ready, 1)

        def down_low(dve):
            dve.wait_ge(w_hi_ready, 3)
            nc.vector.tensor_tensor(down_lo[:].rearrange("p g n -> p (g n)"), st_down,
                                    down_hi[:].rearrange("p g n -> p (g n)"), ALU.subtract).then_inc(w_lo_ready, 1)

        def setup_pe(pe):
            pe.wait_ge(in_fourier, 48)
            nc.tensor.matmul(bank[6][:], fproj_s, fourier_s, start=True, stop=True).then_inc(fenc_ps, 1)

        def norm_stage(steps, n, xb):
            even, odd = stats[:, :, 0:3], stats[:, :, 3:6]
            steps.wait()
            if n == 0:
                for t in range(TT):
                    steps.mark(nc.vector.bn_stats(stats[:, t, :], xb(t)))
            elif n == 1:
                steps.mark(nc.vector.tensor_tensor(mv[:, :, 0], even[:, :, 1], odd[:, :, 1], ALU.add))
                steps.mark(nc.vector.tensor_tensor(mv[:, :, 1], even[:, :, 1], odd[:, :, 1], ALU.subtract))
                steps.mark(nc.vector.tensor_tensor(ve[:], even[:, :, 2], odd[:, :, 2], ALU.add))
            elif n == 2:
                steps.mark(nc.vector.tensor_scalar(mean[:], mv[:, :, 0], 0.5, None, ALU.mult))
                steps.mark(nc.vector.tensor_scalar(rs[:], ve[:], 1.0 / D, EPS, ALU.mult, ALU.add))
                steps.mark(nc.vector.tensor_tensor(nt[:, 0, :], mv[:, :, 1], mv[:, :, 1], ALU.mult))
            elif n == 3:
                steps.mark(nc.vector.scalar_tensor_tensor(ve[:], nt[:, 0, :], 0.25, rs[:], ALU.mult, ALU.add))
            elif n == 4:
                steps.mark(nc.vector.tensor_scalar(rsi[:], ve[:].bitcast(I32), 1, None, ALU.logical_shift_right))
            elif n == 5:
                steps.mark(nc.vector.tensor_scalar(rs[:].bitcast(I32), rsi[:], -1, RSQRT_MAGIC, ALU.mult, ALU.add))
            elif n < LN_STAGES - 1:
                if n % 3 == 0:
                    steps.mark(nc.vector.tensor_tensor(nt[:, 0, :], ve[:], rs[:], ALU.mult))
                    steps.mark(nc.vector.tensor_scalar(nt[:, 2, :], rs[:], -0.5, None, ALU.mult))
                elif n % 3 == 1:
                    steps.mark(nc.vector.tensor_tensor(nt[:, 1, :], nt[:, 0, :], rs[:], ALU.mult))
                else:
                    steps.mark(nc.vector.scalar_tensor_tensor(rs[:], nt[:, 1, :], -3.0, nt[:, 2, :],
                                                              ALU.add, ALU.mult))
            else:
                for t in range(TT):
                    last = nc.vector.tensor_scalar(xn[:, t, :], xb(t), mean[:, t:t + 1], rs[:, t:t + 1],
                                                   ALU.subtract, ALU.mult)
                    if t < TT - 1:
                        steps.mark(last)
                return last

        def layer_norm(steps, xb):
            for n in range(LN_STAGES):
                last = norm_stage(steps, n, xb)
            return last

        def ffn(tag, last, follow=None):
            s = {n: sem(f"{tag}_{n}") for n in (
                "xn_ready", "xt_ps", "x_hi_ready", "x_lo_ready", "logits_t", "logits_copied", "logits",
                "shifted", "exps", "masks", "pos", "comb_parts", "comb_ps", "comb_ready", "gate_ps", "up_ps", "silu",
                "gated", "weight_ps", "hidden", "hid_hi_ready", "hid_lo_ready", "y_ps", "y_copied",
                "yt_ps", "x_done")}
            G, U, C = (bank[0], bank[1]), (bank[2], bank[3]), (bank[4], bank[5])
            Y, M = bank[6], bank[7]
            YT = C[1]
            M_log = M[:, 0:TT * E]
            M_comb = M[0:SPLIT3 * E, 0:T // 2].bitcast(BF16)
            step_sem, route_sem = dve_step[tag], sem(f"{tag}_route_step")
            x2_hi, x2_lo = q_st[:, 0], q_st[:, 1]
            hid = work[:, 4096 + INNER:4096 + INNER + NH * T].rearrange("p (n t) -> p n t", n=NH)
            y_f, log_t = rope_tmp[:, 0, :], rope_tmp[:, 1, :]
            LAG_Y = 4
            OPEN = 4
            NORM_EARLY_AT = {5: range(0, 1), 6: range(1, 4), 7: range(4, 7), 8: range(7, 9), 9: range(9, 11)}
            NORM_AT = {0: range(11, 13), 1: range(13, 15), 2: range(15, 16)}
            NORM_FIRST_AT = {0: range(0, 4), 1: range(4, 10), 2: range(10, 16)}
            ROUTE_EARLY_AT = {6: range(0, 2), 7: range(2, 5), 8: range(5, 6), 9: range(6, 8)}
            ROUTE_AT = {0: range(8, 14), 1: range(14, 20)}
            FRONT_AT, GATE_AT, LOGITS_AT, EXP_AT, POSITIONS_AT, COMBINE_AT = 4, 6, 6, 7, 2, 3

            def groups(eng, step, end, first=0):
                for k in range(first, OPEN):
                    step(0, k, False, True)
                with eng.Fori(0, B - 1) as b:
                    for k in range(OPEN, GROUPS):
                        step(b, k, True, True)
                    for k in range(OPEN):
                        step(b + 1, k, True, True)
                for k in range(OPEN, GROUPS):
                    step(B - 1, k, True, False)
                end(B)

            def group(b, k):
                return b * GROUPS + k

            def behind(b, k, lag):
                return (b, k - lag) if k >= lag else (b - 1, k - lag + GROUPS)

            def of_batch(ap, b):
                return ap[:, bass.ds(b & 1, 1), :].rearrange("p a t -> p (a t)")

            def places(early):
                if early:
                    return bank[6], lambda b: x_hi[:], lambda b: x_lo[:]
                return bank[7], lambda b: of_batch(x2_hi, b), lambda b: of_batch(x2_lo, b)

            def pe(pe, early=False):
                M, xh, xl = places(early)

                def front(b):
                    pe.wait_ge(s["xn_ready"], b + 1)
                    for t in range(TT):
                        ins = nc.tensor.transpose(M[:, t * P:(t + 1) * P], xn[:, t, :], ident[:])
                    ins.then_inc(s["xt_ps"], 1)

                def gate(b):
                    pe.wait_ge(s["x_hi_ready"], b + 1)
                    pe.wait_ge(s["x_lo_ready"], b + 1)
                    for n, (w, x_part) in enumerate(((gate_hi, xh), (gate_hi, xl), (gate_lo, xh))):
                        ins = nc.tensor.matmul(M[0:E, :], w[:], x_part(b), start=(n == 0), stop=(n == 2))
                    ins.then_inc(s["logits_t"], 1)

                def turn_logits(b):
                    pe.wait_ge(s["logits_copied"], b + 1)
                    for t in range(TT):
                        ins = nc.tensor.transpose(M[:, t * P:(t + 1) * P], log_t[:, t * P:(t + 1) * P], ident[:])
                    ins.then_inc(s["logits"], 1)

                def gate_up(b, k, before, more):
                    if k == 0:
                        pe.wait_ge(s["x_lo_ready"], b + 1)
                    for dst, j, read, done in ((G[k % 2], 0, "silu", "gate_ps"),
                                               (U[k % 2], GROUPS, "gated", "up_ps")):
                        if j:
                            between(b, k, before, more)
                        if before or k >= 2:
                            pe.wait_ge(s[read], group(b, k - 1))
                        for n, (w, a) in enumerate(((gu_hi, x2_hi), (gu_lo, x2_hi), (gu_hi, x2_lo))):
                            ins = nc.tensor.matmul(dst[:], w[:, j + k, :], of_batch(a, b),
                                                   start=(n == 0), stop=(n == 2))
                        ins.then_inc(s[done], 1)

                def positions(b):
                    if last and isinstance(b, int) and b == 0:
                        pe.wait_ge(att["x_done"], B)
                    pe.wait_ge(s["masks"], b + 1)
                    nc.tensor.matmul(M_log, before_b[:], mask_b[:].rearrange("p t e -> p (t e)"),
                                     start=True, stop=False)
                    nc.tensor.matmul(M_log.rearrange("p (t e) -> p t e", e=E), ones_b[:],
                                     count_b[:].unsqueeze(1).broadcast_to([P, TT, E]), start=False, stop=False)
                    for t in range(TT - 1):
                        ins = nc.tensor.matmul(
                            M[:, (t + 1) * E:TT * E].rearrange("p (t e) -> p t e", e=E), ones_b[:],
                            mask_b[:, t:t + 1, :].broadcast_to([P, TT - 1 - t, E]), start=False, stop=(t == TT - 2))
                    ins.then_inc(s["pos"], 1)

                def combine_t(b):
                    pe.wait_ge(s["comb_parts"], b + 1)
                    for t in range(TT):
                        ins = nc.tensor.transpose(M_comb[:, t * P:(t + 1) * P],
                                                  comb3[:, t, :, :].rearrange("p a e -> p (a e)"), ident_b[:])
                    ins.then_inc(s["comb_ps"], 1)

                def weights(b, k):
                    e = k - NSH
                    if e == 0:
                        pe.wait_ge(s["comb_ready"], b + 1)
                    if e >= 2:
                        pe.wait_ge(s["hidden"], b * E + (e - 1))
                    if e == 1:
                        pe.wait_ge(s["gated"], group(b, k + 1))
                    nc.tensor.matmul(C[k % 2][:], sel_b[:, e, :], comb_t[:],
                                     start=True, stop=True).then_inc(s["weight_ps"], 1)

                def project(b, k, before):
                    pe.wait_ge(s["hid_lo_ready"], group(b, k + 1))
                    if k == 0 and before:
                        pe.wait_ge(s["y_copied"], b)
                    for n, (w, a) in enumerate(((down_hi, hid_hi), (down_lo, hid_hi), (down_hi, hid_lo))):
                        ins = nc.tensor.matmul(Y[:], w[:, k, :], a[:, k % 2, :], start=(k == 0 and n == 0),
                                               stop=(k == GROUPS - 1 and n == 2))
                    ins.then_inc(s["y_ps"], 1)

                def transpose_y(b):
                    pe.wait_ge(s["y_copied"], b)
                    pe.wait_ge(s["hidden"], b * E)
                    for t in range(TT):
                        ins = nc.tensor.transpose(YT[:, t * P:(t + 1) * P], y_f[:, t * P:(t + 1) * P], ident[:])
                    ins.then_inc(s["yt_ps"], 1)

                def between(b, k, before, more):
                    if k == GATE_AT and more:
                        gate(b + 1)
                    if k < 2 and before:
                        weights(b - 1, GROUPS + k - 2)
                    if k - 2 >= NSH:
                        weights(b, k - 2)
                    if k == POSITIONS_AT:
                        positions(b)
                    if before or k >= LAG_Y:
                        project(*behind(b, k, LAG_Y), before)

                def step(b, k, before, more):
                    gate_up(b, k, before, more)
                    if k == LAG_Y - 1 and not before:
                        pe.wait_ge(w_lo_ready, 3)
                    if k == COMBINE_AT:
                        combine_t(b)
                    if k == 3 and before:
                        transpose_y(b)
                    if follow and not more:
                        follow["tensor"](pe, k)
                    if more:
                        if k == FRONT_AT:
                            front(b + 1)
                        if k == LOGITS_AT:
                            turn_logits(b + 1)

                def end(b):
                    weights(b - 1, GROUPS - 2)
                    weights(b - 1, GROUPS - 1)
                    for k in range(LAG_Y):
                        project(*behind(b, k, LAG_Y), True)
                    transpose_y(b)

                if early:
                    return dict(front=front, gate=gate, turn_logits=turn_logits, gate_up=gate_up)
                if tag == "f1":
                    pe.wait_ge(in_first, 32)
                    front(0)
                    pe.wait_ge(w_lo_ready, 1)
                    gate(0)
                    turn_logits(0)
                    pe.wait_ge(in_small, 16 * 4)
                    pe.wait_ge(consts_ready, 2)
                    pe.wait_ge(w_lo_ready, 2)
                    pe.wait_ge(fenc_ready, 1)
                groups(pe, step, end, 0 if tag == "f1" else EARLY_GROUPS)

            def act(act, early=False):
                M, xh, xl = places(early)

                def x_high(b):
                    act.wait_ge(s["xt_ps"], b + 1)
                    nc.scalar.activation(xh(b), M[:], ACT.Copy).then_inc(s["x_hi_ready"], 1)

                def copy_logits(b):
                    act.wait_ge(s["logits_t"], b + 1)
                    nc.scalar.activation(log_t, M[:], ACT.Copy).then_inc(s["logits_copied"], 1)

                def exponentials(b):
                    act.wait_ge(s["shifted"], b + 1)
                    nc.scalar.activation(route[:, 1], route[:, 0], ACT.Exp).then_inc(s["exps"], 1)

                def silu(b, k, before):
                    act.wait_ge(s["gate_ps"], group(b, k + 1))
                    if before or k >= 2:
                        act.wait_ge(s["gated"], group(b, k - 1))
                    nc.scalar.activation(act_g[:, k % 2, :], G[k % 2][:], ACT.Silu).then_inc(s["silu"], 1)

                def hidden_high(b, k, before):
                    if k < NSH:
                        act.wait_ge(s["gated"], group(b, k + 1))
                    else:
                        act.wait_ge(s["hidden"], b * E + (k - NSH + 1))
                    if before or k >= 2:
                        act.wait_ge(s["y_ps"], group(b, k - 1))
                    nc.scalar.activation(hid_hi[:, k % 2, :], hid[:, k % NH, :], ACT.Copy)\
                      .then_inc(s["hid_hi_ready"], 1)

                def copy_y(b):
                    act.wait_ge(s["y_ps"], b * GROUPS)
                    nc.scalar.activation(y_f, Y[:], ACT.Copy, scale=0.5).then_inc(s["y_copied"], 1)

                def step(b, k, before, more):
                    silu(b, k, before)
                    if more:
                        if k == FRONT_AT:
                            x_high(b + 1)
                        if k == EXP_AT:
                            exponentials(b + 1)
                    if before or k >= 2:
                        hidden_high(*behind(b, k, 2), before)
                    if k == 2 and before:
                        copy_y(b)
                    if more and k == GATE_AT - 1:
                        copy_logits(b + 1)
                    if follow and k == follow["fill_at"]:
                        follow["high"](act, b)
                    if follow and not more:
                        follow["scalar"](act, k)

                def end(b):
                    hidden_high(b - 1, GROUPS - 2, True)
                    hidden_high(b - 1, GROUPS - 1, True)
                    copy_y(b)

                if early:
                    return dict(x_high=x_high, copy_logits=copy_logits, exponentials=exponentials)
                if tag == "f1":
                    x_high(0)
                    ffn_weights_high(act)
                    copy_logits(0)
                    exponentials(0)
                if tag == "f2":
                    act.wait_ge(q_split, B * PAIRS)
                    act.wait_ge(k_own_low, B * PAIRS)
                    act.wait_ge(k_far_high, B * PAIRS)
                groups(act, step, end)

            def dve(dve, early=False):
                M, xh, xl = places(early)
                big, small_t = (lambda n: route[:, n]), (lambda n: small[:, n, :])
                per_e = lambda ap: ap.unsqueeze(2).broadcast_to([P, TT, E])
                logits = M[:].rearrange("p (t c) -> p t c", t=TT)[:, :, 0:E]
                before_it = M_log.rearrange("p (t e) -> p t e", e=E)

                def x_low(b):
                    dve.wait_ge(s["x_hi_ready"], b + 1)
                    nc.vector.tensor_tensor(xl(b), M[:], xh(b),
                                            ALU.subtract).then_inc(s["x_lo_ready"], 1)

                def route_stage(n, b):
                    tt, ts = nc.vector.tensor_tensor, nc.vector.tensor_scalar
                    routed.wait()
                    if n == 0:
                        dve.wait_ge(s["logits"], b + 1)
                        routed.mark(nc.vector.tensor_reduce(small_t(0), logits, AX.X, ALU.max))
                    elif n == 1:
                        tt(big(0), logits, per_e(small_t(0)), ALU.subtract).then_inc(s["shifted"], 1)
                    elif n == 2:
                        dve.wait_ge(s["exps"], b + 1)
                        routed.mark(nc.vector.tensor_reduce(small_t(1), big(1), AX.X, ALU.add))
                    elif n == 3:
                        routed.mark(nc.vector.reciprocal(small_t(2), small_t(1)))
                    elif n == 4:
                        routed.mark(tt(big(2), big(1), per_e(small_t(2)), ALU.mult))
                    elif n == 5:
                        other = big(2).unsqueeze(2).broadcast_to([P, TT, E, E])
                        own = big(2).unsqueeze(3).broadcast_to([P, TT, E, E])
                        routed.mark(tt(pair_gt[:], other, own, ALU.is_gt))
                        routed.mark(tt(pair_ge[:], other, own, ALU.is_ge))
                    elif n == 6:
                        routed.mark(tt(pair_ge[:], pair_ge[:], lower[:].unsqueeze(1).broadcast_to([P, TT, E, E]),
                                      ALU.mult))
                    elif n == 7:
                        routed.mark(tt(pair_gt[:], pair_gt[:], pair_ge[:], ALU.max))
                    elif n == 8:
                        routed.mark(nc.vector.tensor_reduce(big(3), pair_gt[:], AX.X, ALU.add))
                    elif n == 9:
                        ts(mask_b[:], big(3), float(TOPK), None, ALU.is_lt).then_inc(s["masks"], 1)
                    elif n == 10:
                        dve.wait_ge(s["masks"], b + 1)
                        routed.mark(tt(big(4), big(2), mask_b[:], ALU.mult))
                        routed.mark(nc.vector.tensor_reduce(tile_n[:], mask_b[:].rearrange("p t e -> p e t"),
                                                           AX.X, ALU.add))
                    elif n == 11:
                        routed.mark(nc.vector.tensor_reduce(small_t(3), big(4), AX.X, ALU.add))
                    elif n == 12:
                        routed.mark(ts(small_t(4), small_t(3), 1e-20, None, ALU.add))
                    elif n == 13:
                        routed.mark(nc.vector.reciprocal(small_t(5), small_t(4)))
                    elif n == 14:
                        routed.mark(tt(big(5), big(4), per_e(small_t(5)), ALU.mult))
                    elif n == 15:
                        dve.wait_ge(s["pos"], b + 1)
                        routed.mark(nc.vector.scalar_tensor_tensor(big(6), before_it, float(CAPACITY), big(5),
                                                                  ALU.is_lt, ALU.mult))
                        routed.mark(tt(count[:], count[:], tile_n[:], ALU.add))
                    elif n == 16:
                        routed.mark(nc.vector.tensor_copy(comb3[:, :, 0, :], big(6)))
                        routed.mark(nc.vector.tensor_copy(count_b[:], count[:]))
                    elif n == 17:
                        routed.mark(tt(big(7), big(6), comb3[:, :, 0, :], ALU.subtract))
                    elif n == 18:
                        routed.mark(nc.vector.tensor_copy(comb3[:, :, 1, :], big(7)))
                    else:
                        tt(comb3[:, :, 2, :], big(7), comb3[:, :, 1, :], ALU.subtract).then_inc(s["comb_parts"], 1)

                def combine_ready(b, before):
                    dve.wait_ge(s["comb_ps"], b + 1)
                    if before:
                        dve.wait_ge(s["weight_ps"], b * E)
                    nc.vector.tensor_copy(comb_t[0:SPLIT3 * E, :], M_comb).then_inc(s["comb_ready"], 1)

                def gated(b, k, before):
                    dve.wait_ge(s["silu"], group(b, k + 1))
                    dve.wait_ge(s["up_ps"], group(b, k + 1))
                    if k < NSH:
                        if before:
                            dve.wait_ge(s["hid_lo_ready"], group(b, k - NH + 1))
                        dst = hid[:, k % NH, :]
                    else:
                        if before or k >= NSH + 2:
                            dve.wait_ge(s["hidden"], b * E + max(k - NSH - 1, 0))
                        dst = prod[:, k % 2, :]
                    nc.vector.tensor_tensor(dst, act_g[:, k % 2, :], U[k % 2][:],
                                            ALU.mult).then_inc(s["gated"], 1)

                def weighted(b, k):
                    dve.wait_ge(s["weight_ps"], b * E + (k - NSH + 1))
                    dve.wait_ge(s["gated"], group(b, k + 1))
                    if k >= NH:
                        dve.wait_ge(s["hid_lo_ready"], group(b, k - NH + 1))
                    nc.vector.tensor_tensor(hid[:, k % NH, :], prod[:, k % 2, :], C[k % 2][:],
                                            ALU.mult).then_inc(s["hidden"], 1)

                def residual(b):
                    dve.wait_ge(s["yt_ps"], b)
                    xb = x_tok[:, bass.ds(b - 1, 1), :, :].rearrange("p a t d -> p (a t d)")
                    nc.vector.tensor_tensor(xb, YT[:], xb, ALU.add).then_inc(s["x_done"], 1)
                    dve.wait_ge(s["x_done"], b)

                def norm_and_route(norms, b_norm, routes, b_route):
                    for n in range(max(len(norms), len(routes))):
                        if n < len(routes):
                            route_stage(routes[n], b_route)
                        if n < len(norms):
                            ins = norm_stage(steps, norms[n], x_tile(b_norm & (B - 1)))
                            if ins is not None:
                                ins.then_inc(s["xn_ready"], 1)

                def step(b, k, before, more):
                    if k == 3 and before:
                        residual(b)
                    gated(b, k, before)
                    if k == 0 and before:
                        weighted(b - 1, GROUPS - 1)
                    if k - 1 >= NSH:
                        weighted(b, k - 1)
                    if k == 0 and not before and tag == "f1":
                        down_low(dve)
                        dve.wait_ge(in_x, 16 * (B - 1))
                    if more:
                        if k == FRONT_AT:
                            x_low(b + 1)
                        norm_and_route(NORM_EARLY_AT.get(k, ()), b + 2, ROUTE_EARLY_AT.get(k, ()), b + 1)
                        norm_and_route((NORM_AT if before else NORM_FIRST_AT).get(k, ()), b + 1,
                                       ROUTE_AT.get(k, ()), b)
                    if k == COMBINE_AT - 1:
                        combine_ready(b, before)
                    if follow and k == follow["fill_at"]:
                        follow["low"](dve, b)
                    if follow and not more:
                        follow["vector"](dve, k)

                def end(b):
                    weighted(b - 1, GROUPS - 1)
                    residual(b)

                steps, routed = Steps(dve, step_sem), Steps(dve, route_sem)
                if tag == "f1" or early:
                    routed.mark(nc.vector.memset(count[:], 0.0))
                    routed.mark(nc.vector.memset(count_b[:], 0.0))
                if early:
                    return dict(x_low=x_low, route_stage=route_stage, routed=routed)
                if tag == "f1":
                    dve.wait_ge(in_x0, 16)
                    layer_norm(steps, lambda t: x_tok[:, 0, t, :]).then_inc(s["xn_ready"], 1)
                    gate_low(dve)
                    x_low(0)
                    gate_up_low(dve)
                    route_stage(0, 0)
                    route_stage(1, 0)
                    dve.wait_ge(in_small, 16 * 4)
                    dve.wait_ge(w_lo_ready, 2)
                else:
                    steps.n, routed.n = LN_STEPS, early_routed[0]
                if tag == "f1":
                    for k in (7, 8, 9):
                        norm_and_route((), 1, ROUTE_EARLY_AT[k], 0)
                for k in range(OPEN):
                    step(0, k, False, True)
                first, first_routed = steps.n, routed.n
                with dve.Fori(0, B - 1) as b:
                    steps = Steps(dve, step_sem, b * LN_STEPS + first)
                    routed = Steps(dve, route_sem, b * ROUTE_STEPS + first_routed)
                    for k in range(OPEN, GROUPS):
                        step(b, k, True, True)
                    for k in range(OPEN):
                        step(b + 1, k, True, True)
                    assert (steps.n, routed.n) == (LN_STEPS, ROUTE_STEPS), (steps.n, routed.n)
                for k in range(OPEN, GROUPS):
                    step(B - 1, k, True, False)
                end(B)

            def pool(pool):
                def hidden_low(b, k, before):
                    pool.wait_ge(s["hid_hi_ready"], group(b, k + 1))
                    if before or k >= 2:
                        pool.wait_ge(s["y_ps"], group(b, k - 1))
                    nc.gpsimd.tensor_tensor(hid_lo[:, k % 2, :], hid[:, k % NH, :], hid_hi[:, k % 2, :],
                                            ALU.subtract).then_inc(s["hid_lo_ready"], 1)

                for k in range(2):
                    hidden_low(0, k, False)
                with pool.Fori(0, B - 1) as b:
                    for k in range(2, GROUPS):
                        hidden_low(b, k, True)
                    for k in range(2):
                        hidden_low(b + 1, k, True)
                for k in range(2, GROUPS):
                    hidden_low(B - 1, k, True)

            def sync(sp):
                if last:
                    with sp.Fori(0, B) as b:
                        sp.wait_ge(s["x_done"], b + 1)
                        sp.dma_start(out[bass.ds(b, 1)].rearrange("a (t p) d -> p (a t) d", p=P),
                                     x_tok[:, bass.ds(b, 1)].rearrange("p a t d -> p (a t) d")).then_inc(stored, 16)
                    sp.wait_ge(stored, 16 * B)

            early_steps = []

            def early_norm(dve, n):
                if n == 0:
                    early_steps.append(Steps(dve, step_sem))
                ins = norm_stage(early_steps[0], n, lambda t: x_tok[:, 0, t, :])
                if ins is not None:
                    ins.then_inc(s["xn_ready"], 1)
            return dict(tensor=pe, scalar=act, vector=dve, gpsimd=pool, sync=sync, early_norm=early_norm, x_done=s["x_done"],
                        xn_ready=s["xn_ready"])

        def attention():
            s = {n: sem(f"att_{n}") for n in (
                "xn_ready", "xt_ps", "x_hi_ready", "x_lo_ready", "qk_ps", "roped", "added", "own_high",
                "v_ps", "v_ready", "scores", "maxes", "probs", "pt_ps", "pt_ready", "o_ps",
                "rec_ready", "rec_t_ps", "rec_t_ready", "rec_ps", "rec_copied", "o_ready",
                "y_ps", "y_copied", "yt_ps", "x_done")}
            S, PT = (bank[0], bank[1]), (bank[2], bank[3])
            O, R, J, Y = bank[4], bank[5], bank[6], bank[7]
            R_t = R[0:SPLIT3 * UNITS, 0:P // 2].bitcast(BF16)
            y_end = rope_tmp[:, 0, :]
            rec_t = comb_t[:, 0:P]
            step_sem, pool_step = dve_step["att"], sem("pool_step")
            ORDER = (2, 3, 0, 1)
            OWN = (slice(0, DH), slice(DH, P))
            FAR = (slice(DH, P), slice(0, DH))
            PARTS_AT = {0: (0,), 1: (1,), 2: (2, 3)}
            PART_BANK = (J, R, J, R)
            V_BANK = (Y, O, PT[0], PT[1])
            PV_AT = {3: 0, 4: 1, 5: 2, 7: 3}
            V_AT = (3, 4, 5, 6)
            V_PAIR = {PAIRS - 1: 0, 2: 1}
            OPEN = 3
            FRONT_PAIR, FRONT_UNIT = PAIRS - 2, 4
            NORM_AT = [(j, u) for j in range(OPEN, FRONT_PAIR) for u in (1, 3, 5, 6, 7)] + [(FRONT_PAIR, 1)]
            REC_STEPS = 5
            nothing = lambda b, j: None

            W_ALL = 3 + PAIRS + 2

            FILL_AT = 5
            EARLY_FRONT = 5
            EARLY_PARTS = {7: 0, 8: 1}

            def early_pe(pe, k):
                if k in EARLY_PARTS:
                    i = EARLY_PARTS[k]
                    pe.wait_ge(w_lo_ready, 4)
                    pe.wait_ge(s["x_lo_ready"], 1)
                    if i:
                        pe.wait_ge(s["roped"], i)
                    for n, (w, a) in enumerate(((qk_hi, x_hi), (qk_lo, x_hi), (qk_hi, x_lo))):
                        ins = nc.tensor.matmul(Y[:], w[:, 0, ORDER[i], :], a[:], start=(n == 0), stop=(n == 2))
                    ins.then_inc(s["qk_ps"], 1)
                if k == EARLY_FRONT:
                    pe.wait_ge(ffn1["xn_ready"], B + 1)
                    for t in range(TT):
                        ins = nc.tensor.transpose(Y[:, t * P:(t + 1) * P], xn[:, t, :], ident[:])
                    ins.then_inc(s["xt_ps"], 1)

            def qk_high(act, b):
                act.wait_ge(in_att, 16 * 5)
                pair = bass.ds(b, 1)
                nc.scalar.activation(qk_hi[:, pair, 2:4], st_qk[:, pair, 2:4], ACT.Copy)
                nc.scalar.activation(qk_hi[:, pair, 0:2], st_qk[:, pair, 0:2], ACT.Copy,
                                     scale=QSCALE).then_inc(w_hi_ready, 1)

            def qk_low(dve, b):
                dve.wait_ge(w_hi_ready, b + 4)
                pair = bass.ds(b, 1)
                nc.vector.tensor_tensor(qk_lo[:, pair, 2:4], st_qk[:, pair, 2:4], qk_hi[:, pair, 2:4], ALU.subtract)
                nc.vector.scalar_tensor_tensor(qk_lo[:, pair, 0:2], st_qk[:, pair, 0:2], QSCALE,
                                               qk_hi[:, pair, 0:2], ALU.mult, ALU.subtract).then_inc(w_lo_ready, 1)

            def early_act(act, k):
                if k in (FILL_AT + 1, FILL_AT + 2):
                    cols = slice((k - FILL_AT - 1) * T, (k - FILL_AT) * T)
                    nc.scalar.activation(v_hi[:, cols], st_v[:, cols], ACT.Copy).then_inc(w_hi_ready, 1)
                if k == EARLY_FRONT:
                    act.wait_ge(s["xt_ps"], 1)
                    nc.scalar.activation(x_hi[:], Y[:], ACT.Copy).then_inc(s["x_hi_ready"], 1)

            def early_dve(dve, k):
                if k in (FILL_AT + 1, FILL_AT + 2):
                    cols = slice((k - FILL_AT - 1) * T, (k - FILL_AT) * T)
                    dve.wait_ge(w_hi_ready, 3 + PAIRS + k - FILL_AT)
                    nc.vector.tensor_tensor(v_lo[:, cols], st_v[:, cols], v_hi[:, cols],
                                            ALU.subtract).then_inc(w_lo_ready, 1)
                if k == EARLY_FRONT:
                    dve.wait_ge(s["x_hi_ready"], 1)
                    nc.vector.tensor_tensor(x_lo[:], Y[:], x_hi[:], ALU.subtract).then_inc(s["x_lo_ready"], 1)
                if k in EARLY_PARTS:
                    i = EARLY_PARTS[k]
                    dve.wait_ge(s["qk_ps"], i + 1)
                    nc.vector.tensor_tensor(rope_tmp[:, ORDER[i], :], Y[:], rope_t[:, ORDER[i] % 2, :],
                                            ALU.mult).then_inc(s["roped"], 1)

            def pairs(eng, pair, end):
                for j in range(OPEN):
                    pair(0, j, min(j, 2), True)
                with eng.Fori(0, B - 1) as b:
                    for j in range(OPEN, PAIRS):
                        pair(b, j, 2, True)
                    for j in range(OPEN):
                        pair(b + 1, j, 2, True)
                for j in range(OPEN, PAIRS):
                    pair(B - 1, j, 2, False)
                end(B - 1)

            def unit_of(b, j, u):
                return b * (PAIRS * UNITS) + (j * UNITS + u)

            def pe(pe):
                def front(b):
                    pe.wait_ge(s["xn_ready"], b)
                    for t in range(TT):
                        ins = nc.tensor.transpose(J[:, t * P:(t + 1) * P], xn[:, t, :], ident[:])
                    ins.then_inc(s["xt_ps"], 1)

                def roped(b, j, i):
                    pe.wait_ge(s["roped"], b * (PAIRS * PARTS) + (j * PARTS + i + 1))

                def project(b, j, i):
                    if i >= 2:
                        roped(b, j, i - 2)
                    for n, (w, a) in enumerate(((qk_hi, x_hi), (qk_lo, x_hi), (qk_hi, x_lo))):
                        ins = nc.tensor.matmul(PART_BANK[i][:], w[:, j % PAIRS, ORDER[i], :], a[:],
                                               start=(n == 0), stop=(n == 2))
                    ins.then_inc(s["qk_ps"], 1)

                def values(b, half, t, to=J):
                    if t and to is J:
                        pe.wait_ge(s["v_ready"], b * (2 * TT) + (half * TT + t))
                    cols = slice(half * T, (half + 1) * T)
                    tok = slice(t * P, (t + 1) * P)
                    for n, (a, w) in enumerate(((x_hi, v_hi), (x_lo, v_hi), (x_hi, v_lo))):
                        ins = nc.tensor.matmul(to[:], a[:, tok], w[:, cols], start=(n == 0), stop=(n == 2))
                    ins.then_inc(s["v_ps"], 1)

                def scores(b, j, u, first):
                    h, qt = divmod(u, TT)
                    if u == 0:
                        pe.wait_ge(q_split, b * PAIRS + (j + 1))
                        pe.wait_ge(k_own_low, b * PAIRS + (j + 1))
                        pe.wait_ge(k_far_high, b * PAIRS + (j + 1))
                    if not first or u >= 2:
                        pe.wait_ge(s["probs"], unit_of(b, j, u - 1))
                    for i, k in enumerate((k_hh, k_ll)):
                        ins = nc.tensor.matmul(S[u % 2][:], q_st[:, j % 2, h, qt * P:(qt + 1) * P],
                                               k[:, j % 2, h, :], start=(i == 0), stop=(i == 1))
                    ins.then_inc(s["scores"], 1)

                def transposes(b, j, u, first=False):
                    pe.wait_ge(s["probs"], unit_of(b, j, u + 1))
                    if not first or u >= 2:
                        pe.wait_ge(s["pt_ready"], unit_of(b, j, u - 1))
                    for k in range(TT):
                        ins = nc.tensor.transpose(PT[u % 2][:, k * P:(k + 1) * P],
                                                  prob[:, u % NP, k * P:(k + 1) * P], ident[:])
                    ins.then_inc(s["pt_ps"], 1)

                def apply_v(b, j, k, first=False):
                    if k == 0:
                        pe.wait_ge(s["pt_ready"], unit_of(b, j + 1, 0))
                        if not first:
                            pe.wait_ge(s["o_ready"], b * PAIRS + j)
                    for h in range(2):
                        n = 2 * (j % PAIRS) + h
                        ins = nc.tensor.matmul(O[h * DH:(h + 1) * DH, :], v_all[:, k, n * DH:(n + 1) * DH],
                                               pt[:, j % 2, h, k, :], start=(k == 0), stop=(k == TT - 1))
                    if k == TT - 1:
                        ins.then_inc(s["o_ps"], 1)

                def transpose_reciprocals(b, j):
                    pe.wait_ge(s["rec_ready"], b * PAIRS + (j + 1))
                    nc.tensor.transpose(R_t, rec3[:, j % 2].rearrange("p a h t -> p (a h t)"), ident_b[:])\
                      .then_inc(s["rec_t_ps"], 1)

                def reciprocals(b, j):
                    pe.wait_ge(s["rec_t_ready"], b * PAIRS + (j + 1))
                    for qt in range(TT):
                        for h in range(2):
                            ins = nc.tensor.matmul(R[h * DH:(h + 1) * DH, qt * P:(qt + 1) * P],
                                                   sel_b[:, h * TT + qt, 0:DH], rec_t, start=True, stop=True)
                    ins.then_inc(s["rec_ps"], 1)

                def project_out(b, j):
                    pe.wait_ge(s["o_ready"], b * PAIRS + (j + 1))
                    j = j % PAIRS
                    nc.tensor.matmul(Y[:], wo[:, j, :], o_t[:, j % 2, :], start=(j == 0),
                                     stop=(j == PAIRS - 1)).then_inc(s["y_ps"], 1)

                def transpose_y(b, y):
                    pe.wait_ge(s["y_copied"], b)
                    for t in range(TT):
                        ins = nc.tensor.transpose(Y[:, t * P:(t + 1) * P], y[:, t * P:(t + 1) * P], ident[:])
                    ins.then_inc(s["yt_ps"], 1)

                ffn_early = ffn2["tensor"](pe, early=True)

                def pair(b, j, before, more):
                    nxt = more or j < PAIRS - 1
                    batch_before = not (isinstance(b, int) and b == 0)
                    for u in range(UNITS):
                        scores(b, j, u, before == 0)
                        if not more and (j, u) == (FRONT_PAIR, FRONT_UNIT):
                            roped(b, j + 1, 2)
                            ffn_early["front"](0)
                        if not more and (j, u) == (FRONT_PAIR, FRONT_UNIT + 2):
                            ffn_early["gate"](0)
                        if not more and (j, u) == (FRONT_PAIR + 1, 3):
                            ffn_early["turn_logits"](0)
                        if nxt:
                            if u == 0 and j == PAIRS - 1:
                                pe.wait_ge(s["x_lo_ready"], b + 2)
                            if u == 0 and j in (0, 3):
                                pe.wait_ge(s["v_ready"], b * (2 * TT) + (TT if j == 0 else 2 * TT))
                            if u == 1 and before == 2:
                                pe.wait_ge(s["rec_copied"], b * PAIRS + (j - 1))
                            for i in PARTS_AT.get(u, ()):
                                project(b, j + 1, i)
                        if (j, u) == (FRONT_PAIR, FRONT_UNIT) and more:
                            roped(b, j + 1, 2)
                            front(b + 1)
                        if j in V_PAIR and u in V_AT and (more or j != PAIRS - 1):
                            if u == V_AT[0]:
                                roped(b, j + 1, 2)
                            values(b + 1 if j == PAIRS - 1 else b, V_PAIR[j], V_AT.index(u))
                        if u >= LAG:
                            transposes(b, j, u - LAG, before == 0)
                        elif before:
                            transposes(b, j - 1, UNITS - LAG + u)
                        if before and u in PV_AT:
                            apply_v(b, j - 1, PV_AT[u], before == 1)
                        if before and u == 5:
                            if nxt:
                                roped(b, j + 1, 3)
                            transpose_reciprocals(b, j - 1)
                        if before == 2 and u == 6:
                            if j == 2 and batch_before:
                                pe.wait_ge(s["x_done"], b)
                            project_out(b, j - 2)
                        if before and u == 6:
                            reciprocals(b, j - 1)
                        if j == 2 and u == 1 and batch_before:
                            transpose_y(b, y_t)

                def end(b):
                    j = PAIRS - 1
                    for u in range(UNITS - LAG, UNITS):
                        transposes(b, j, u)
                    pe.wait_ge(s["rec_copied"], b * PAIRS + j)
                    transpose_reciprocals(b, j)
                    project_out(b, j - 1)
                    for k in range(TT):
                        apply_v(b, j, k)
                    reciprocals(b, j)
                    pe.wait_ge(x_moved, 2)
                    ffn_early["gate_up"](0, 0, False, True)
                    project_out(b, j)
                    ffn_early["gate_up"](0, 1, False, True)
                    transpose_y(b + 1, y_end)

                pe.wait_ge(w_lo_ready, W_ALL)
                pe.wait_ge(s["x_lo_ready"], 1)
                for i in range(len(EARLY_PARTS), PARTS):
                    if PART_BANK[i] is R:
                        pe.wait_ge(ffn1["x_done"], B)
                    project(0, 0, i)
                for t in range(TT):
                    values(0, 0, t, V_BANK[t])
                pairs(pe, pair, end)

            def act(act):
                def x_high(b):
                    act.wait_ge(s["xt_ps"], b + 1)
                    nc.scalar.activation(x_hi[:], J[:], ACT.Copy).then_inc(s["x_hi_ready"], 1)

                def values(b, half, t, of=J):
                    act.wait_ge(s["v_ps"], b * (2 * TT) + (half * TT + t + 1))
                    nc.scalar.activation(v_all[:, t, half * T:(half + 1) * T], of[:], ACT.Copy)\
                      .then_inc(s["v_ready"], 1)

                def exponentials(b, j, u, first):
                    act.wait_ge(s["maxes"], unit_of(b, j, u + 1))
                    if not first or u >= NP:
                        act.wait_ge(s["pt_ps"], unit_of(b, j, u + 1 - NP))
                    nc.scalar.activation(prob[:, u % NP, :], S[u % 2][:], ACT.Exp,
                                         bias=neg_max[:, j % 2, u:u + 1],
                                         accum_out=den[:, j % 2, u:u + 1]).then_inc(s["probs"], 1)

                def move(b, j, u):
                    h, qt = divmod(u, TT)
                    act.wait_ge(s["pt_ps"], unit_of(b, j, u + 1))
                    nc.scalar.activation(pt[:, j % 2, h, :, qt * P:(qt + 1) * P],
                                         PT[u % 2][:].rearrange("p (k q) -> p k q", q=P),
                                         ACT.Copy).then_inc(s["pt_ready"], 1)

                def far_high(b, j):
                    act.wait_ge(s["added"], b * (2 * PAIRS) + (2 * j + 1))
                    for h in range(2):
                        ins = nc.scalar.activation(k_hh[FAR[h], j % 2, h, :], rope_tmp[OWN[h], 2, :], ACT.Copy)
                    ins.then_inc(k_far_high, 1)

                def copy_reciprocals(b, j):
                    act.wait_ge(s["rec_t_ps"], b * PAIRS + (j + 1))
                    nc.scalar.activation(rec_t[0:SPLIT3 * UNITS, :], R_t, ACT.Copy).then_inc(s["rec_t_ready"], 1)

                def spread_reciprocals(b, j, before):
                    act.wait_ge(s["rec_ps"], b * PAIRS + (j + 1))
                    if before == 2:
                        act.wait_ge(s["o_ready"], b * PAIRS + j)
                    nc.scalar.activation(rec_all[:], R[:], ACT.Copy).then_inc(s["rec_copied"], 1)

                def copy_y(b, to):
                    act.wait_ge(s["y_ps"], b * PAIRS)
                    nc.scalar.activation(to, Y[:], ACT.Identity, bias=bo[:, 0:1]).then_inc(s["y_copied"], 1)

                ffn_early = ffn2["scalar"](act, early=True)

                def pair(b, j, before, more):
                    nxt = more or j < PAIRS - 1
                    batch_before = not (isinstance(b, int) and b == 0)
                    for u in range(UNITS):
                        exponentials(b, j, u, before == 0)
                        if not more and (j, u) == (FRONT_PAIR, FRONT_UNIT):
                            ffn_early["x_high"](0)
                        if not more and (j, u) == (FRONT_PAIR + 1, 1):
                            act.wait_ge(q_split, B * PAIRS)
                            act.wait_ge(k_own_low, B * PAIRS)
                            ffn_early["copy_logits"](0)
                        if not more and (j, u) == (FRONT_PAIR + 1, 4):
                            ffn_early["exponentials"](0)
                            nc.scalar.activation(q_st[:, 0, 0, :], x_hi[:], ACT.Copy).then_inc(x_moved, 1)
                        if j in V_PAIR and u in V_AT and (more or j != PAIRS - 1):
                            values(b + 1 if j == PAIRS - 1 else b, V_PAIR[j], V_AT.index(u))
                        if (j, u) == (FRONT_PAIR, FRONT_UNIT) and more:
                            x_high(b + 1)
                        if u >= LAG:
                            move(b, j, u - LAG)
                        elif before:
                            move(b, j - 1, UNITS - LAG + u)
                        if before and u == 5:
                            copy_reciprocals(b, j - 1)
                        if before and u == 7:
                            spread_reciprocals(b, j - 1, before)
                        if nxt and u == 3:
                            far_high(b, j + 1)
                        if j == 1 and u == 7 and batch_before:
                            copy_y(b, y_t)

                def end(b):
                    j = PAIRS - 1
                    for u in range(UNITS - LAG, UNITS):
                        move(b, j, u)
                    copy_reciprocals(b, j)
                    spread_reciprocals(b, j, 2)
                    copy_y(b + 1, y_end)

                act.wait_ge(w_lo_ready, W_ALL)
                far_high(0, 0)
                for t in range(TT):
                    values(0, 0, t, V_BANK[t])
                pairs(act, pair, end)

            def dve(dve):
                def x_low(b):
                    dve.wait_ge(s["x_hi_ready"], b + 1)
                    nc.vector.tensor_tensor(x_lo[:], J[:], x_hi[:], ALU.subtract).then_inc(s["x_lo_ready"], 1)

                def rope_part(b, j, i):
                    dve.wait_ge(s["qk_ps"], b * (PAIRS * PARTS) + (j * PARTS + i + 1))
                    nc.vector.tensor_tensor(rope_tmp[:, ORDER[i], :], PART_BANK[i][:], rope_t[:, ORDER[i] % 2, :],
                                            ALU.mult).then_inc(s["roped"], 1)

                def k_own_high(b, j):
                    dve.wait_ge(s["added"], b * (2 * PAIRS) + (2 * j + 1))
                    for h in range(2):
                        ins = nc.vector.tensor_copy(k_hh[OWN[h], j % 2, h, :], rope_tmp[OWN[h], 2, :])
                    ins.then_inc(s["own_high"], 1)

                def k_far_low(b, j):
                    dve.wait_ge(s["own_high"], b * PAIRS + (j + 1))
                    for h in range(2):
                        steps.mark(nc.vector.tensor_tensor(k_ll[FAR[h], j % 2, h, :], rope_tmp[OWN[h], 2, :],
                                                           k_hh[OWN[h], j % 2, h, :], ALU.subtract))

                def q_high(b, j):
                    dve.wait_ge(s["added"], b * (2 * PAIRS) + (2 * j + 2))
                    for h in range(2):
                        steps.mark(nc.vector.tensor_copy(q_st[OWN[h], j % 2, h, :], rope_tmp[OWN[h], 0, :]))

                def q_low(b, j):
                    steps.wait()
                    for h in range(2):
                        ins = nc.vector.tensor_tensor(q_st[FAR[h], j % 2, h, :], rope_tmp[OWN[h], 0, :],
                                                      q_st[OWN[h], j % 2, h, :], ALU.subtract)
                    ins.then_inc(q_split, 1)

                def maxima(b, j, u):
                    dve.wait_ge(s["scores"], unit_of(b, j, u + 1))
                    nc.vector.tensor_reduce(neg_max[:, j % 2, u:u + 1], S[u % 2][:], AX.X, ALU.max,
                                            negate=True).then_inc(s["maxes"], 1)

                def reciprocals(b, j, n):
                    parts = [rec3[:, j % 2, a].rearrange("p h t -> p (h t)") for a in range(SPLIT3)]
                    steps.wait()
                    if n == 0:
                        dve.wait_ge(s["probs"], unit_of(b, j + 1, 0))
                        steps.mark(nc.vector.reciprocal(rec[:, 0, :], den[:, j % 2, :]))
                    elif n == 1:
                        steps.mark(nc.vector.tensor_copy(parts[0], rec[:, 0, :]))
                    elif n == 2:
                        steps.mark(nc.vector.tensor_tensor(rec[:, 1, :], rec[:, 0, :], parts[0], ALU.subtract))
                    elif n == 3:
                        steps.mark(nc.vector.tensor_copy(parts[1], rec[:, 1, :]))
                    else:
                        nc.vector.tensor_tensor(parts[2], rec[:, 1, :], parts[1],
                                                ALU.subtract).then_inc(s["rec_ready"], 1)

                def normalise(b, j):
                    dve.wait_ge(s["o_ps"], b * PAIRS + (j + 1))
                    dve.wait_ge(s["rec_copied"], b * PAIRS + (j + 1))
                    nc.vector.tensor_tensor(o_t[:, j % 2, :], O[:], rec_all[:], ALU.mult).then_inc(s["o_ready"], 1)

                def residual(b):
                    dve.wait_ge(s["yt_ps"], b)
                    which = slice(b - 1, b) if isinstance(b, int) else bass.ds(b - 1, 1)
                    xb = x_tok[:, which, :, :].rearrange("p a t d -> p (a t d)")
                    nc.vector.tensor_tensor(xb, Y[:], xb, ALU.add).then_inc(s["x_done"], 1)
                    dve.wait_ge(s["x_done"], b)

                ffn_early = {}
                ROUTE_AT = {3: (0, 1), 5: (2, 3), 6: (4, 5), 7: (6, 7)}

                def pair(b, j, before, more):
                    nxt = more or j < PAIRS - 1
                    batch_before = not (isinstance(b, int) and b == 0)
                    for u in range(UNITS):
                        maxima(b, j, u)
                        if not more and (j, u) == (FRONT_PAIR, FRONT_UNIT):
                            ffn_early.update(ffn2["vector"](dve, early=True))
                            ffn_early["x_low"](0)
                        if not more and j == FRONT_PAIR + 1:
                            for n in ROUTE_AT.get(u, ()):
                                ffn_early["route_stage"](n, 0)
                        if before and 1 <= u < REC_STEPS:
                            reciprocals(b, j - 1, u)
                        if nxt:
                            for i in PARTS_AT.get(u, ()):
                                rope_part(b, j + 1, i)
                            {3: k_own_high, 4: k_far_low, 5: q_high, 6: q_low}.get(u, nothing)(b, j + 1)
                        if before == 2 and u == 0:
                            normalise(b, j - 2)
                        if before and u == 0:
                            reciprocals(b, j - 1, 0)
                        if (j, u) == (FRONT_PAIR, FRONT_UNIT) and more:
                            x_low(b + 1)
                        if j == 2 and u == 2 and batch_before:
                            residual(b)
                        if more and (j, u) in NORM_AT:
                            ins = norm_stage(steps, NORM_AT.index((j, u)), x_tile(b + 1))
                            if ins is not None:
                                ins.then_inc(s["xn_ready"], 1)
                        if not more and (j, u) in NORM_AT:
                            ffn2["early_norm"](dve, NORM_AT.index((j, u)))

                def end(b):
                    j = PAIRS - 1
                    early_routed.append(ffn_early["routed"].n)
                    nc.vector.tensor_copy(q_st[:, 1, 0, :], x_lo[:]).then_inc(x_moved, 1)
                    normalise(b, j - 1)
                    for n in range(REC_STEPS):
                        reciprocals(b, j, n)
                    normalise(b, j)
                    residual(b + 1)

                assert len(NORM_AT) == LN_STAGES
                steps = Steps(dve, step_sem)
                for i in range(len(EARLY_PARTS), PARTS):
                    rope_part(0, 0, i)
                k_own_high(0, 0)
                k_far_low(0, 0)
                q_high(0, 0)
                q_low(0, 0)
                for j in range(OPEN):
                    pair(0, j, min(j, 2), True)
                first = steps.n
                per = LN_STEPS + (REC_STEPS - 1 + 4) * PAIRS
                with dve.Fori(0, B - 1) as b:
                    steps = Steps(dve, step_sem, b * per + first)
                    for j in range(OPEN, PAIRS):
                        pair(b, j, 2, True)
                    for j in range(OPEN):
                        pair(b + 1, j, 2, True)
                    assert steps.n == per, (steps.n, per)
                steps = Steps(dve, step_sem, (B - 1) * per + first)
                for j in range(OPEN, PAIRS):
                    pair(B - 1, j, 2, False)
                end(B - 1)

            def pool(pool):
                def rotate(g, parity):
                    tmp = lambda part: rope_tmp[:, part, :]
                    steps = Steps(pool, pool_step, g * 3)
                    pool.wait_ge(s["roped"], g * PARTS + 2)
                    steps.link(nc.gpsimd.tensor_tensor(tmp(3), tmp(3), fenc[:, 1, :], ALU.add))
                    nc.gpsimd.tensor_tensor(tmp(2), tmp(2), tmp(3), ALU.add).then_inc(s["added"], 1)
                    pool.wait_ge(s["roped"], g * PARTS + PARTS)
                    steps.link(nc.gpsimd.tensor_tensor(tmp(1), tmp(1), fenc[:, 0, :], ALU.add))
                    nc.gpsimd.tensor_tensor(tmp(0), tmp(0), tmp(1), ALU.add).then_inc(s["added"], 1)
                    pool.wait_ge(s["added"], g * 2 + 2)
                    pool.wait_ge(s["own_high"], g + 1)
                    steps.link(nc.gpsimd.tensor_tensor(k_ll[OWN[0], parity, 0, :], tmp(2)[OWN[0]],
                                                       k_hh[OWN[0], parity, 0, :], ALU.subtract))
                    nc.gpsimd.tensor_tensor(k_ll[OWN[1], parity, 1, :], tmp(2)[OWN[1]],
                                            k_hh[OWN[1], parity, 1, :], ALU.subtract).then_inc(k_own_low, 1)
                    pool.wait_ge(k_own_low, g + 1)

                pool.wait_ge(fenc_ready, 2)
                with pool.Fori(0, B * PAIRS // 2) as two:
                    rotate(two * 2, 0)
                    rotate(two * 2 + 1, 1)
            return dict(tensor=pe, scalar=act, vector=dve, gpsimd=pool, x_done=s["x_done"],
                        early=dict(tensor=early_pe, scalar=early_act, vector=early_dve, fill_at=FILL_AT,
                                   high=qk_high, low=qk_low))

        def x_tile(b):
            return lambda t: x_tok[:, bass.ds(b, 1), t, :].rearrange("p a d -> p (a d)")

        early_routed = []
        att = attention()
        ffn1, ffn2 = ffn("f1", False, follow=att["early"]), ffn("f2", True)

        @block.sync
        def _(sp):
            setup_sync(sp)
            ffn2["sync"](sp)

        @block.scalar
        def _(act):
            setup_act(act)
            ffn1["scalar"](act)
            att["scalar"](act)
            ffn2["scalar"](act)

        @block.vector
        def _(dve):
            setup_dve(dve)
            ffn1["vector"](dve)
            att["vector"](dve)
            ffn2["vector"](dve)

        @block.tensor
        def _(pe):
            setup_pe(pe)
            ffn1["tensor"](pe)
            att["tensor"](pe)
            ffn2["tensor"](pe)

        @block.gpsimd
        def _(pool):
            ffn1["gpsimd"](pool)
            att["gpsimd"](pool)
            ffn2["gpsimd"](pool)


def kernel(L0_attn_x, L0_attn_w_qkv, L0_attn_w_fproj, L0_attn_b_fproj, L0_attn_w_out, L0_attn_b_out,
           L0_ffn_gate_w, L0_ffn_we_gate, L0_ffn_we_up, L0_ffn_we_down, L0_ffn_ws_gate, L0_ffn_ws_up,
           L0_ffn_ws_down):
    import ml_dtypes
    import numpy as np
    import concourse.bacc as bacc
    from concourse.bass_utils import run_bass_kernel_spmd

    a = np.asarray
    wqkv = a(L0_attn_w_qkv).reshape(3, HEADS, DH, D)
    half = DH // 2
    turned = np.r_[2 * np.arange(half) + 1, 2 * np.arange(half)]
    qk = np.stack([wqkv[0], wqkv[0][:, turned], wqkv[1], wqkv[1][:, turned]])
    qk = qk.reshape(PARTS, PAIRS, P, D).transpose(3, 1, 0, 2)
    gate = np.concatenate([a(L0_ffn_ws_gate).reshape(NSH, P, D), a(L0_ffn_we_gate)])
    up = np.concatenate([a(L0_ffn_ws_up).reshape(NSH, P, D), a(L0_ffn_we_up)])
    ws_down = a(L0_ffn_ws_down).reshape(D, NSH, P).transpose(2, 1, 0)
    we_down = a(L0_ffn_we_down).transpose(2, 0, 1)
    fproj = a(L0_attn_w_fproj).T

    freqs = np.float32(10000.0) ** (-np.arange(0, DH, 2, dtype=np.float32) / np.float32(DH))
    pos = np.arange(T, dtype=np.float32)
    angles = (pos[:, None] * freqs[None, :]).astype(np.float32).astype(np.float64)
    cos = np.repeat(np.cos(angles), 2, axis=1).T
    sin = np.repeat(np.sin(angles), 2, axis=1).T * np.where(np.arange(DH) < half, -1.0, 1.0)[:, None]
    rope = np.stack([cos, sin]).astype(np.float32)
    rope = np.concatenate([rope, rope], axis=1).transpose(1, 0, 2)
    nf = np.arange(1, NF // 2 + 1, dtype=np.float32)
    fa = (nf[:, None] * pos[None, :]).astype(np.float64)
    fourier = np.concatenate([np.sin(fa), np.cos(fa)]).astype(np.float32)
    ident = np.eye(P, dtype=np.float32)
    lower = np.zeros((P, P), np.float32)
    lower[:, :E * E] = (np.arange(E)[None, :] < np.arange(E)[:, None]).reshape(-1)
    before = np.triu(np.ones((P, P), np.float32), 1)
    sel = np.zeros((P, E, P), np.float32)
    for r in range(SPLIT3 * E):
        sel[r, r % E] = 1.0

    bf = ml_dtypes.bfloat16
    arrays = {
        "x": a(L0_attn_x),
        "w_gate_up": np.concatenate([gate, up]).transpose(2, 0, 1).reshape(P, -1),
        "w_down": np.concatenate([ws_down, we_down], axis=1).reshape(P, -1),
        "gate_t": a(L0_ffn_gate_w).T,
        "w_qk": qk.reshape(P, -1),
        "w_v": wqkv[2].reshape(INNER, D).T,
        "w_out": a(L0_attn_w_out).reshape(D, PAIRS, P).transpose(2, 1, 0).reshape(P, -1),
        "b_out": a(L0_attn_b_out)[:, None],
        "fproj": np.concatenate([fproj, fproj], axis=1),
        "bproj": np.concatenate([a(L0_attn_b_fproj)] * 2)[:, None],
        "rope": rope.reshape(P, -1),
        "fourier": fourier,
        "consts": np.stack([ident, lower]),
        "consts_b": np.stack([before, ident]).astype(bf),
        "sel": sel.reshape(P, -1).astype(bf),
    }
    nc = bacc.Bacc("TRN2", target_bir_lowering=False, num_devices=1)
    inputs, args = {}, []
    for name, v in arrays.items():
        v = np.ascontiguousarray(v)
        inputs[f"in_{name}"] = v
        args.append(nc.dram_tensor(f"in_{name}", v.shape, mybir.dt.from_np(v.dtype), kind="ExternalInput").ap())
    out = nc.dram_tensor("out", (B, T, D), F32, kind="ExternalOutput").ap()
    macaron(nc, *args, out)
    r = run_bass_kernel_spmd(nc, [inputs], core_ids=[0])
    return r.results[0]["out"]
```
